# Optimizing a Trainium2 kernel written in Bass

```python
import numpy as np
import jax
import jax.numpy as jnp

def _softmax(x, axis=-1):
    return jax.nn.softmax(x, axis=axis)

def _gelu(x):
    return jax.nn.gelu(x, approximate=True)

def _silu(x):
    return jax.nn.silu(x)

def _sigmoid(x):
    return jax.nn.sigmoid(x)

def _layernorm(x, axis=-1, eps=1e-05):
    m = jnp.mean(x, axis=axis, keepdims=True)
    v = jnp.var(x, axis=axis, keepdims=True)
    return (x - m) / jnp.sqrt(v + eps)

def _scatter_add(tgt, idx, src, axis=0):
    return tgt.at[idx].add(src)

def _segment_sum(src, seg, n):
    return jax.ops.segment_sum(src, seg, n)
kernel_name = 'mk_sandwich_d1_jaxref_r8_7fdab2'

def setup_inputs(seed: int=0):
    np.random.seed(seed)
    _w = jnp.asarray

    def _L0_attn_setup():
        import jax, jax.numpy as jnp
        import numpy as np
        B, T, C, R = (8, 128, 128, 64)
        EPS = 1e-05
        key = jax.random.key(seed)
        ks = jax.random.split(key, 8)
        x = jax.random.normal(ks[0], (B, T, C), dtype=jnp.float32)
        W_attn = jax.random.normal(ks[1], (3 * C, C), dtype=jnp.float32) * 0.02
        W_proj = jax.random.normal(ks[2], (C, C), dtype=jnp.float32) * 0.02
        lora_attn_A = jax.random.normal(ks[3], (C, R), dtype=jnp.float32) * 0.02
        lora_attn_B = jax.random.normal(ks[4], (R, 3 * C), dtype=jnp.float32) * 0.02
        lora_proj_A = jax.random.normal(ks[5], (C, R), dtype=jnp.float32) * 0.02
        lora_proj_B = jax.random.normal(ks[6], (R, C), dtype=jnp.float32) * 0.02
        bn_gamma = jnp.ones((3 * C,), dtype=jnp.float32)
        bn_beta = jnp.zeros((3 * C,), dtype=jnp.float32)
        return {'x': x, 'W_attn': W_attn, 'W_proj': W_proj, 'lora_attn_A': lora_attn_A, 'lora_attn_B': lora_attn_B, 'lora_proj_A': lora_proj_A, 'lora_proj_B': lora_proj_B, 'bn_gamma': bn_gamma, 'bn_beta': bn_beta}
    _L0_attn_in = _L0_attn_setup()

    def _L0_ffn_setup():
        import jax, jax.numpy as jnp
        import numpy as np
        E = 16
        F_C = 2.0
        D = 128
        I = 4 * D
        IS = 2 * D
        B, S = (4, 128)
        key = jax.random.key(seed)
        ks = jax.random.split(key, 8)
        w = 0.02
        return {'hidden_states': jax.random.normal(ks[0], (B, S, D), dtype=jnp.float32), 'gate_w': jax.random.normal(ks[1], (E, D), dtype=jnp.float32) * w, 'Wg': jax.random.normal(ks[2], (E, I, D), dtype=jnp.float32) * w, 'Wu': jax.random.normal(ks[3], (E, I, D), dtype=jnp.float32) * w, 'Wd': jax.random.normal(ks[4], (E, D, I), dtype=jnp.float32) * w, 'Sg': jax.random.normal(ks[5], (IS, D), dtype=jnp.float32) * w, 'Su': jax.random.normal(ks[6], (IS, D), dtype=jnp.float32) * w, 'Sd': jax.random.normal(ks[7], (D, IS), dtype=jnp.float32) * w}
    _L0_ffn_in = _L0_ffn_setup()
    _d = {'L0_attn_x': _L0_attn_in['x'], 'L0_attn_W_attn': _L0_attn_in['W_attn'], 'L0_attn_W_proj': _L0_attn_in['W_proj'], 'L0_attn_lora_attn_A': _L0_attn_in['lora_attn_A'], 'L0_attn_lora_attn_B': _L0_attn_in['lora_attn_B'], 'L0_attn_lora_proj_A': _L0_attn_in['lora_proj_A'], 'L0_attn_lora_proj_B': _L0_attn_in['lora_proj_B'], 'L0_attn_bn_gamma': _L0_attn_in['bn_gamma'], 'L0_attn_bn_beta': _L0_attn_in['bn_beta'], 'L0_ffn_gate_w': _L0_ffn_in['gate_w'], 'L0_ffn_Wg': _L0_ffn_in['Wg'], 'L0_ffn_Wu': _L0_ffn_in['Wu'], 'L0_ffn_Wd': _L0_ffn_in['Wd'], 'L0_ffn_Sg': _L0_ffn_in['Sg'], 'L0_ffn_Su': _L0_ffn_in['Su'], 'L0_ffn_Sd': _L0_ffn_in['Sd']}
    _x0 = _d['L0_attn_x']
    _d['L0_attn_x'] = jax.random.normal(jax.random.fold_in(jax.random.key(seed), 1), (16, 256, 128), dtype=_x0.dtype)
    del _x0
    return _d

def reference(L0_attn_x, L0_attn_W_attn, L0_attn_W_proj, L0_attn_lora_attn_A, L0_attn_lora_attn_B, L0_attn_lora_proj_A, L0_attn_lora_proj_B, L0_attn_bn_gamma, L0_attn_bn_beta, L0_ffn_gate_w, L0_ffn_Wg, L0_ffn_Wu, L0_ffn_Wd, L0_ffn_Sg, L0_ffn_Su, L0_ffn_Sd):

    def _L0_attn_ref(x, W_attn, W_proj, lora_attn_A, lora_attn_B, lora_proj_A, lora_proj_B, bn_gamma, bn_beta):
        import jax, jax.numpy as jnp
        import numpy as np
        B, T, C, R = (8, 128, 128, 64)
        EPS = 1e-05
        Bb, Tt, Cc = x.shape
        Wm_attn = W_attn + (lora_attn_A @ lora_attn_B).reshape(W_attn.shape)
        xa = jnp.einsum('btc,dc->btd', x, Wm_attn)
        mean = xa.mean(axis=(0, 1))
        var = xa.var(axis=(0, 1))
        xa = (xa - mean) * jax.lax.rsqrt(var + EPS) * bn_gamma + bn_beta
        q, k, v = jnp.split(xa, 3, axis=-1)
        scale = 1.0 / jnp.sqrt(jnp.asarray(Cc, dtype=x.dtype))
        att = jnp.einsum('btc,bsc->bts', q, k) * scale
        causal = jnp.tril(jnp.ones((Tt, Tt), dtype=bool))
        att = jnp.where(causal[None, :, :], att, -jnp.inf)
        att = jax.nn.softmax(att, axis=-1)
        y = jnp.einsum('bts,bsc->btc', att, v)
        y = jnp.einsum('btc,dc->btd', y, W_proj)
        Wm_proj = W_proj + (lora_proj_A @ lora_proj_B).reshape(W_proj.shape)
        y = jnp.einsum('btc,dc->btd', y, Wm_proj)
        return y

    def _L0_ffn_ref(hidden_states, gate_w, Wg, Wu, Wd, Sg, Su, Sd):
        import jax, jax.numpy as jnp
        import numpy as np
        E = 16
        F_C = 2.0
        D = 128
        I = 4 * D
        IS = 2 * D
        B, S = (4, 128)
        b, s, d = hidden_states.shape
        T = b * s
        C = int(T * F_C / E)
        flat_x = hidden_states.reshape(T, d)
        logits = flat_x @ gate_w.T
        scores = jax.nn.softmax(logits, axis=-1).T
        topk_weight, topk_idx = jax.lax.top_k(scores, C)
        xg = flat_x[topk_idx]
        g = jnp.einsum('ecd,eid->eci', xg, Wg)
        u = jnp.einsum('ecd,eid->eci', xg, Wu)
        h = jax.nn.gelu(g, approximate=False) * u
        eo = jnp.einsum('eci,edi->ecd', h, Wd)
        eo = eo * topk_weight[..., None]
        flat_out = jnp.zeros_like(flat_x).at[topk_idx.reshape(-1)].add(eo.reshape(-1, d))
        out = flat_out.reshape(b, s, d)
        sg = hidden_states @ Sg.T
        su = hidden_states @ Su.T
        shared = jax.nn.gelu(sg, approximate=False) * su @ Sd.T
        return out + shared
    x = L0_attn_x
    x = x + _layernorm(_L0_attn_ref(_layernorm(x, axis=-1), L0_attn_W_attn, L0_attn_W_proj, L0_attn_lora_attn_A, L0_attn_lora_attn_B, L0_attn_lora_proj_A, L0_attn_lora_proj_B, L0_attn_bn_gamma, L0_attn_bn_beta), axis=-1)
    x = x + _layernorm(_L0_ffn_ref(_layernorm(x, axis=-1), L0_ffn_gate_w, L0_ffn_Wg, L0_ffn_Wu, L0_ffn_Wd, L0_ffn_Sg, L0_ffn_Su, L0_ffn_Sd), axis=-1)
    return x

_drawn_inputs = setup_inputs


def setup_inputs(seed=0):
    import zlib

    import numpy as np

    out = dict(_drawn_inputs(seed))
    spreads = {'L0_attn_bn_gamma': (1.0, 0.2), 'L0_attn_bn_beta': (0.0, 0.1)}
    factors = {}
    for name, (base, spread) in spreads.items():
        noise = np.random.default_rng([zlib.crc32(name.encode()), seed]).standard_normal(out[name].shape)
        drawn = base * np.exp(spread * noise) if base else spread * noise
        out[name] = jnp.asarray(drawn.astype(out[name].dtype))
    for name, factor in factors.items():
        out[name] = (out[name] * factor).astype(out[name].dtype)
    return out
```

```python
from contextlib import ExitStack

import concourse.bass as bass
from concourse import mybir

F32 = mybir.dt.float32
BF16 = mybir.dt.bfloat16
F16 = mybir.dt.float16
I32 = mybir.dt.int32
ALU = mybir.AluOpType
ACT = mybir.ActivationFunctionType
AX = mybir.AxisListType.X

P = 128
EPS = 1e-5
MASKED = -1.0e30
ds = bass.ds


def pipeline(eng, body, steps, lo, hi, turn=2):
    for n in range(lo):
        body(n // turn, n % turn)
    with eng.Fori(lo // turn, hi // turn) as h:
        for k in range(turn):
            body(h, k)
    for n in range(hi, steps):
        body(n // turn, n % turn)


def stage(h, k, behind, count, turn=2):
    n = turn * h + k - behind
    if isinstance(n, int) and not 0 <= n < count:
        return None
    return n, h + (k - behind) // turn, (k - behind) % turn


def need(eng, semaphore, value):
    if not isinstance(value, int) or value > 0:
        eng.wait_ge(semaphore, value)


def build(nc, x, low_rank_in, attn_w_in, ffn_w_in, w_experts, out):
    TOK = x.shape[0]
    D = x.shape[1]
    NT = TOK // P
    B = TOK // 256
    R = low_rank_in.shape[0]
    E = w_experts.shape[0]
    CAP = TOK * 2 // E
    NS = CAP // P
    IC = w_experts.shape[2] // (3 * P)
    GU = 2 * IC * P
    SC = (ffn_w_in.shape[1] - E) // (3 * P)
    NG = TOK // 512
    NCH = TOK // P
    ROW = D + E
    DIGITS = 15
    FOUR_BIT = 21
    LEFT = (2 * DIGITS - 2 - FOUR_BIT) // 2 + 1
    SCALE = float(D) ** -0.5
    W_UP = 64.0
    assert D == P and CAP == 512 and E * 8 == P and NCH * E == 512 and NG * 2 == DIGITS + 1

    table = nc.dram_tensor("token_table", [TOK, ROW], F32, kind="Internal").ap()
    acc = nc.dram_tensor("ffn_sum", [TOK, D], F32, kind="Internal").ap()

    with ExitStack() as ctx:
        def sb(name, shape, dt=F32):
            return ctx.enter_context(nc.sbuf_tensor(name, shape, dt))

        def sem(name):
            return ctx.enter_context(nc.semaphore(name))

        bank = [ctx.enter_context(nc.psum_tensor(f"bank{i}", [P, 512], F32)) for i in range(8)]

        x_sb = sb("x_sb", [P, NT, D])
        xT = sb("xT", [P, TOK])
        ident = sb("ident", [P, P])
        ident16 = sb("ident16", [P, P], BF16)
        causal = sb("causal", [P, 384], BF16)
        ones16 = sb("ones16", [P, P], F16)
        before = sb("before", [P, P], F16)
        differ = sb("differ", [P, P], F16)
        shift = sb("shift", [P, P], F16)
        same_expert = sb("same_expert", [P, P])
        neg_half = sb("neg_half", [P, 4])
        slot_row = sb("slot_row", [P, CAP], F16)
        slot_col = sb("slot_col", [P, NS, 32])
        scan_keep = sb("scan_keep", [P, E, 32])
        digits = sb("digits", [P, DIGITS + 1, 3], I32)
        digit_shift = sb("digit_shift", [P, DIGITS + 1, 3], I32)
        digit_clamped = sb("digit_clamped", [P, DIGITS + 1, 3], I32)
        digit_bits = sb("digit_bits", [P, DIGITS + 1, 3], I32)
        digit_flip = sb("digit_flip", [P, DIGITS, 3], I32)
        place_shift = sb("place_shift", [P, 2, DIGITS, 3], I32)
        four = sb("four", [P, DIGITS, 3])
        four_bits = sb("four_bits", [P, DIGITS, 3], I32)

        low_rank = sb("low_rank", [R, 6 * P])
        aat, ab = low_rank[:, 0:P], low_rank[:, P:4 * P]
        pat, pb = low_rank[:, 4 * P:5 * P], low_rank[:, 5 * P:6 * P]
        attn_w = sb("attn_w", [P, 4 * D + 6])
        wa, wp = attn_w[:, 0:3 * D], attn_w[:, 3 * D:4 * D]
        gamma, beta = attn_w[:, 4 * D:4 * D + 3], attn_w[:, 4 * D + 3:4 * D + 6]
        wm_raw = sb("wm_raw", [P, 3 * D])
        wmT = sb("wmT", [P, 3 * D])
        wn = sb("wn", [P, 3, D])
        wmp = sb("wmp", [P, D])
        wmpT = sb("wmpT", [P, D])
        p2T = sb("p2T", [P, D])
        gram = sb("gram", [P, D + 1])
        wgram = sb("wgram", [P, 3 * D])
        bn = sb("bn", [P, 8, 3])
        wns = sb("wns", [P, 3, D])
        bv_wide = sb("bv_wide", [P, P])
        mix = sb("mix", [P, D])
        mix_bias = sb("mix_bias", [P, 1])
        p2T_raw = sb("p2T_raw", [P, D])
        p2T_mean = sb("p2T_mean", [P, 1])
        outw = sb("outw", [P, 2, D])
        ones = sb("ones", [P, P])

        xn = sb("xn", [P, 2, 4, D + 1])
        stat = sb("stat", [P, 2, 4, 6])
        mv = sb("mv", [P, 2, 4, 2])
        veps = sb("veps", [P, 2, 4])
        rstd = sb("rstd", [P, 2, 4])
        shiftm = sb("shiftm", [P, 2, 4])

        xT_now = sb("xT_now", [P, 2, 256])
        vals = sb("vals", [P, 2, 256])
        zT = sb("zT", [P, 2, 256])
        top = sb("top", [P, 2, 2])
        nbias = sb("nbias", [P, 2, 2])
        probs = sb("probs", [P, 2, 384])
        psums = sb("psums", [P, 2, 2])
        rsums = sb("rsums", [P, 2, 2])
        probsT = sb("probsT", [P, 2, 384])
        f = sb("f", [P, 2, 2, D])
        stat2 = sb("stat2", [P, 2, 4, 6])
        mv2 = sb("mv2", [P, 2, 4, 2])
        veps2 = sb("veps2", [P, 2, 4])
        rstd2 = sb("rstd2", [P, 2, 4])
        shift2 = sb("shift2", [P, 2, 2])
        xr = sb("xr", [P, 2, 2, D])
        xrT = sb("xrT", [P, 2, 256])

        ffn_w = sb("ffn_w", [P, 3 * SC * P + E])
        sg, su = ffn_w[:, 0:SC * P], ffn_w[:, SC * P:2 * SC * P]
        sd = ffn_w[:, 2 * SC * P:3 * SC * P].rearrange("p (c d) -> p c d", d=D)
        gate = ffn_w[:, 3 * SC * P:]
        logit = sb("logit", [P, NT, E])
        rmax = sb("rmax", [P, NT])
        rsum = sb("rsum", [P, NT])
        rinv = sb("rinv", [P, NT])
        score = sb("score", [P, NT, E])
        by_expert = sb("by_expert", [P, 512])
        hits = sb("hits", [P, 3, 512], BF16)
        cand = sb("cand", [P, 2, 3], I32)
        cand_next = sb("cand_next", [P, 3], I32)
        enough = sb("enough", [P, 7])
        four_plus_digit = sb("four_plus_digit", [P, 1])
        count = sb("count", [P, 7])
        least_wide = sb("least_wide", [P, P])
        least = sb("least", [P, E])
        chunked = sb("chunked", [P, 32, E])
        above = sb("above", [P, E, 32])
        equal = sb("equal", [P, E, 32])
        above_sum = sb("above_sum", [P, E, 32], F16)
        equal_sum = sb("equal_sum", [P, E, 32], F16)
        equal_taken = sb("equal_taken", [P, E, 32], F16)
        wanted = sb("wanted", [P, E])
        equal_before = sb("equal_before", [P, E])
        wanted_here = sb("wanted_here", [P, E])
        chunk_base = sb("chunk_base", [P, E], F16)
        rank_steps = sb("rank_steps", [P, E, 33], F16)
        first_rank = sb("first_rank", [P, E])
        started = sb("started", [P, 2, CAP], F16)
        passed = sb("passed", [P, NS, 32])
        passed_sum = sb("passed_sum", [P, NS])
        idx_f = sb("idx_f", [P, NS])
        idx_in = sb("idx_in", [P, 4, NS], I32)
        idx_out = sb("idx_out", [P, 4, NS], I32)

        sgelu = sb("sgelu", [P, SC, 512])
        sup = sb("sup", [P, SC, 512])
        shid = sb("shid", [P, 2, SC, 512])
        sout = sb("sout", [P, 2, 4, D])

        w_gu = sb("w_gu", [P, 2, GU])
        w_gu_hi = sb("w_gu_hi", [P, 2, GU], F16)
        w_gu_lo = sb("w_gu_lo", [P, 2, GU], F16)
        w_down = sb("w_down", [P, 2, IC * P])
        xg = sb("xg", [P, 2, NS, ROW])
        weight = sb("weight", [P, 4, NS])
        xgT_hi = sb("xgT_hi", [P, 2, CAP], F16)
        xgT_lo = sb("xgT_lo", [P, 2, CAP], F16)
        gelu = sb("gelu", [P, 2, CAP])
        hid = sb("hid", [P, 2, IC, CAP])
        eo = sb("eo", [P, 2, NS, D])

        attn_loaded = sem("attn_loaded")
        ffn_loaded = sem("ffn_loaded")
        x_loaded = [sem(f"x_loaded{i}") for i in range(4)]
        dve_waited = sem("dve_waited")
        pool_waited = sem("pool_waited")
        consts_step = sem("consts_step")
        consts_ready = sem("consts_ready")
        prep_pe = sem("prep_pe")
        prep_act = sem("prep_act")
        ln1_step = sem("ln1_step")
        ln1_var = sem("ln1_var")
        ln1_rstd = sem("ln1_rstd")
        ln1_shift = sem("ln1_shift")
        ln1_done = sem("ln1_done")
        ln1_done_act = sem("ln1_done_act")
        ln1_turned = sem("ln1_turned")
        ln1_used = sem("ln1_used")
        xT_ready = sem("xT_ready")
        fold_pe = sem("fold_pe")
        fold_dve = sem("fold_dve")
        fold_pow = sem("fold_pow")
        fold_mean = sem("fold_mean")
        z_done = sem("z_done")
        z_copied = sem("z_copied")
        scores_done = sem("scores_done")
        max_step = sem("max_step")
        exp_done = sem("exp_done")
        rsums_done = sem("rsums_done")
        probs_turned = sem("probs_turned")
        probsT_ready = sem("probsT_ready")
        xT_now_loaded = [sem(f"xT_now_loaded{i}") for i in range(2)]
        vals_done = sem("vals_done")
        vals_copied = sem("vals_copied")
        f_done = sem("f_done")
        f_ready = sem("f_ready")
        f_stats = sem("f_stats")
        x2_ready = sem("x2_ready")
        x2_stats = sem("x2_stats")
        norm_aggr = sem("norm_aggr")
        norm_var = sem("norm_var")
        norm_pow = sem("norm_pow")
        shift_ready = sem("shift_ready")
        xr_ready = sem("xr_ready")
        xr_stored = [sem(f"xr_stored{i}") for i in range(2)]
        xr_turned = sem("xr_turned")
        xrT_ready = sem("xrT_ready")
        xrT_kept = [sem(f"xrT_kept{i}") for i in range(2)]
        logits_done = sem("logits_done")
        soft_dve = sem("soft_dve")
        soft_exp = sem("soft_exp")
        score_stored = sem("score_stored")
        chunks_loaded = sem("chunks_loaded")
        score_turned = sem("score_turned")
        by_expert_ready = sem("by_expert_ready")
        counted = sem("counted")
        counts_summed = sem("counts_summed")
        search_step = sem("search_step")
        sh_gate_done = sem("sh_gate_done")
        sh_up_done = sem("sh_up_done")
        sh_gelu = sem("sh_gelu")
        sh_up = sem("sh_up")
        sh_hid = sem("sh_hid")
        sh_out_done = sem("sh_out_done")
        sh_out_copied = sem("sh_out_copied")
        sh_stored = [sem(f"sh_stored{i}") for i in range(2)]
        rank_dve = sem("rank_dve")
        rank_pe = sem("rank_pe")
        rank_act = sem("rank_act")
        gu_loaded = [sem(f"gu_loaded{i}") for i in range(2)]
        down_loaded = [sem(f"down_loaded{i}") for i in range(2)]
        gu_hi_ready = sem("gu_hi_ready")
        gu_lo_ready = sem("gu_lo_ready")
        started_ready = sem("started_ready")
        looked_up = sem("looked_up")
        idx_step = sem("idx_step")
        gathered = [sem(f"gathered{i}") for i in range(2)]
        xg_turned = sem("xg_turned")
        xgT_hi_ready = sem("xgT_hi_ready")
        xgT_lo_ready = sem("xgT_lo_ready")
        kept = sem("kept")
        gate_done = sem("gate_done")
        up_done = sem("up_done")
        gelu_done = sem("gelu_done")
        hid_done = sem("hid_done")
        eo_done = sem("eo_done")
        tail_done = sem("tail_done")
        tail_scaled = sem("tail_scaled")
        eo_scaled = sem("eo_scaled")
        scattered = [sem(f"scattered{i}") for i in range(2)]
        sum_loaded = [sem(f"sum_loaded{i}") for i in range(4)]
        fin_step = sem("fin_step")
        fin_var = sem("fin_var")
        fin_pow = sem("fin_pow")
        fin_shift = sem("fin_shift")
        fin_normed = sem("fin_normed")
        fin_ready_pool = sem("fin_ready_pool")
        fin_ready_dve = sem("fin_ready_dve")
        stored = sem("stored")

        PER_MAX, PER_IDX = 3, 4
        A_STEPS, A_LO, A_HI = B + 6, 8, B - 2
        E_TURN, E_LO, E_HI = 4, 4, E - 4

        x_v = x.rearrange("(t q) d -> q t d", q=P)
        out_v = out.rearrange("(t q) d -> q t d", q=P)
        acc_v = acc.rearrange("(t q) d -> q t d", q=P)
        table_v = table.rearrange("(t q) r -> q t r", q=P)
        acc_sb = xT[:, :].rearrange("p (t d) -> p t d", d=D)

        block = ctx.enter_context(nc.Block())

        @block.sync
        def _(sp):
            for g in range(NG):
                if g >= 4:
                    sp.wait_ge(x_loaded[g % 4], 16 * (g // 4))
                sp.dma_start(x_sb[:, 4 * g:4 * g + 4, :], x_v[:, 4 * g:4 * g + 4, :]).then_inc(x_loaded[g % 4], 16)
            for e in range(2):
                sp.dma_start(w_gu[:, e, :], w_experts[e, :, 0:GU]).then_inc(gu_loaded[e], 16)
            for e in range(2):
                sp.dma_start(w_down[:, e, :], w_experts[e, :, GU:]).then_inc(down_loaded[e], 16)

            def load_now(n, k):
                need(sp, vals_done, n - 1)
                sp.dma_start(xT_now[:, k, :], xT[:, ds(256 * n, 256)]).then_inc(xT_now_loaded[k], 16)

            def body(h, k):
                if s := stage(h, k, -1, B):
                    load_now(s[0], s[2])
                if s := stage(h, k, 4, B):
                    n, _, kk = s
                    sp.wait_ge(xr_ready, n + 1)
                    sp.dma_start(table_v[:, ds(2 * n, 2), 0:D], xr[:, kk, :, :]).then_inc(xr_stored[kk], 16)
                if s := stage(h, k, 5, B):
                    n, _, kk = s
                    sp.wait_ge(xrT_ready, n + 1)
                    sp.dma_start(xT[:, ds(256 * n, 256)], xrT[:, kk, :]).then_inc(xrT_kept[kk], 16)

            sp.wait_ge(xT_ready, NG)
            load_now(0, 0)
            pipeline(sp, body, A_STEPS, A_LO, A_HI)

            sp.wait_ge(soft_dve, 5)
            sp.dma_start(table_v[:, :, D:ROW], score[:, :, :]).then_inc(score_stored, 16)
            sp.wait_ge(score_stored, 16)
            sp.dma_start(chunked[:, :, :],
                         table.rearrange("(p j) r -> p j r", j=32)[:, :, D:ROW]).then_inc(chunks_loaded, 16)
            with sp.Fori(0, NG // 2) as h:
                for k in range(2):
                    g = 2 * h + k
                    sp.wait_ge(sh_out_copied, g + 1)
                    sp.dma_start(acc_v[:, ds(4 * g, 4), :], sout[:, k, :, :]).then_inc(sh_stored[k], 16)
            def load_gate_up(e, k):
                sp.wait_ge(gu_hi_ready, e - 1)
                sp.wait_ge(gu_lo_ready, e - 1)
                sp.dma_start(w_gu[:, k, :], w_experts[ds(e, 1), :, 0:GU].rearrange("a p n -> p (a n)")
                             ).then_inc(gu_loaded[k], 16)

            def load_down(e, k):
                sp.wait_ge(eo_done, e - 1)
                sp.dma_start(w_down[:, k, :], w_experts[ds(e, 1), :, GU:].rearrange("a p n -> p (a n)")
                             ).then_inc(down_loaded[k], 16)

            load_gate_up(2, 0)
            with sp.Fori(1, E // 2 - 1) as h:
                for k in range(2):
                    load_gate_up(2 * h + k + 1, 1 - k)
                    load_down(2 * h + k, k)
            load_gate_up(E - 1, 1)
            load_down(E - 2, 0)
            load_down(E - 1, 1)
            for k in range(2):
                sp.wait_ge(scattered[k], 16 * NS * (E // 2))
            for g in range(NG):
                if g >= 4:
                    sp.wait_ge(sum_loaded[g % 4], 16 * (g // 4))
                sp.dma_start(acc_sb[:, 4 * g:4 * g + 4, :], acc_v[:, 4 * g:4 * g + 4, :]).then_inc(sum_loaded[g % 4], 16)
            for g in range(NG):
                sp.wait_ge(fin_ready_pool, g + 1)
                sp.wait_ge(fin_ready_dve, g + 1)
                sp.dma_start(out_v[:, 4 * g:4 * g + 4, :], x_sb[:, 4 * g:4 * g + 4, :]).then_inc(stored, 16)
            sp.wait_ge(stored, 16 * NG)

        @block.gpsimd
        def _(pool):
            done = [0]

            def step(ins):
                done[0] += 1
                ins.then_inc(consts_step, 1)
                pool.wait_ge(consts_step, done[0])

            def diagonal(tile, value, base, fill_where=ALU.not_equal):
                return nc.gpsimd.affine_select(out=tile, in_=tile, compare_op=fill_where, fill=value, base=base,
                                               pattern=[[-1, tile.shape[-1]]], channel_multiplier=1)

            step(nc.gpsimd.memset(neg_half[:], -0.5))
            step(nc.gpsimd.memset(ident[:], 0.0))
            step(diagonal(ident[:, :], 1.0, 0))
            step(nc.gpsimd.tensor_copy(ident16[:], ident[:]))
            step(nc.gpsimd.memset(causal[:], 0.0))
            for lo in (0, 256):
                step(nc.gpsimd.affine_select(out=causal[:, lo:lo + P], in_=causal[:, lo:lo + P], compare_op=ALU.is_ge,
                                             fill=MASKED, base=0, pattern=[[-1, P]], channel_multiplier=1))
            step(nc.gpsimd.memset(ones16[:], 1.0))
            nc.gpsimd.memset(ones[:], 1.0).then_inc(consts_ready, 1)

            def first(h, k):
                if s := stage(h, k, 0, NG):
                    g = s[0]
                    pool.wait_ge(ln1_var, g + 1)
                    need(pool, ln1_done_act, 2 * (g - 1))
                    nc.gpsimd.tensor_tensor(rstd[:, k, :], veps[:, k, :], neg_half[:, :],
                                            ALU.pow).then_inc(ln1_rstd, 1)

            pipeline(pool, first, NG, 2, NG)
            pool.wait_ge(fold_dve, 7)
            nc.gpsimd.tensor_tensor(bn[:, 5, :], bn[:, 4, :], neg_half[:, 0:3], ALU.pow).then_inc(fold_pow, 1)

            step(nc.gpsimd.affine_select(out=before[:, :], in_=ones16[:, :], compare_op=ALU.is_gt, fill=0.0, base=0,
                                         pattern=[[1, P]], channel_multiplier=-1))
            step(nc.gpsimd.memset(shift[:], 0.0))
            step(diagonal(shift[:, :], 1.0, 1))
            step(nc.gpsimd.memset(differ[:], 0.0))
            step(diagonal(differ[:, :], 1.0, 0))
            step(diagonal(differ[:, :], -1.0, 1))
            step(nc.gpsimd.memset(same_expert[:], 0.0))
            for off in range(-(P // E) + 1, P // E):
                step(diagonal(same_expert[:, :], 1.0, E * off))
            step(nc.gpsimd.iota(digits[:], pattern=[[0, DIGITS + 1], [1, 3]], base=1, channel_multiplier=0))
            step(nc.gpsimd.iota(digit_shift[:], pattern=[[-2, DIGITS + 1], [0, 3]], base=2 * DIGITS - 2,
                                channel_multiplier=0))
            step(nc.gpsimd.iota(place_shift[:, 0, :, :], pattern=[[-2, DIGITS], [0, 3]], base=2 * DIGITS - 2 - FOUR_BIT,
                                channel_multiplier=0))
            step(nc.gpsimd.iota(place_shift[:, 1, :, :], pattern=[[2, DIGITS], [0, 3]], base=FOUR_BIT - 2 * DIGITS + 2,
                                channel_multiplier=0))
            step(nc.gpsimd.memset(four[:], 4.0))
            step(nc.gpsimd.iota(slot_row[:], pattern=[[1, CAP]], base=0, channel_multiplier=0,
                                allow_small_or_imprecise_dtypes=True))
            step(nc.gpsimd.iota(slot_col[:], pattern=[[P, NS], [0, 32]], base=0, channel_multiplier=1,
                                allow_small_or_imprecise_dtypes=True))
            step(nc.gpsimd.memset(scan_keep[:], 1.0))
            step(nc.gpsimd.memset(scan_keep[:, :, 0:1], 0.0))
            nc.gpsimd.memset(rank_steps[:, :, 32:33], 1.0).then_inc(consts_ready, 1)

            def body(h, k):
                if s := stage(h, k, 2, B + 2):
                    n, _, kk = s
                    pool.wait_ge(norm_var, n + 1)
                    need(pool, xr_ready, n - 2)
                    nc.gpsimd.tensor_tensor(rstd2[:, kk, :], veps2[:, kk, :], neg_half[:, :],
                                            ALU.pow).then_inc(norm_pow, 1)

            pipeline(pool, body, A_STEPS, A_LO, A_HI)

            with pool.Fori(0, NG // 2) as h:
                for k in range(2):
                    g = 2 * h + k
                    for c in range(SC):
                        pool.wait_ge(sh_gelu, SC * g + c + 1)
                        pool.wait_ge(sh_up, SC * g + c + 1)
                        nc.gpsimd.tensor_tensor(shid[:, k, c, :], sgelu[:, c, :], sup[:, c, :],
                                                ALU.mult).then_inc(sh_hid, 1)

            def gather(s):
                n, _, k4 = s
                k = k4 % 2
                pool.wait_ge(score_stored, 16)
                pool.wait_ge(idx_step, PER_IDX * (n + 1))
                need(pool, xg_turned, n - 1)
                need(pool, kept, n - 1)
                pool.sem_inc(pool_waited, 1)
                for t in range(NS):
                    nc.gpsimd.indirect_dma_start(
                        out=xg[:, k, t, :], out_offset=None, in_=table[:, :],
                        in_offset=bass.IndirectOffsetOnAxis(ap=idx_in[:, k4, t:t + 1], axis=0)).then_inc(gathered[k], 16)

            def scatter(s):
                n, h, k4 = s
                k, pair = k4 % 2, 2 * h + k4 // 2
                for g in range(2):
                    pool.wait_ge(sh_stored[g], 16 * (NG // 2))
                tail = isinstance(n, int) and n == E - 1
                if not tail:
                    pool.wait_ge(eo_scaled, 2 * (n + 1))
                if k == 0:
                    need(pool, scattered[1], 16 * NS * pair)
                else:
                    pool.wait_ge(scattered[0], 16 * NS * (pair + 1))
                pool.sem_inc(pool_waited, 1)
                for t in range(NS):
                    if tail:
                        pool.wait_ge(tail_scaled, t + 2)
                    nc.gpsimd.indirect_dma_start(
                        out=acc[:, :], out_offset=bass.IndirectOffsetOnAxis(ap=idx_out[:, k4, t:t + 1], axis=0),
                        in_=eo[:, k, t, :], in_offset=None, compute_op=ALU.add).then_inc(scattered[k], 16)

            def experts(h, k):
                if s := stage(h, k, -2, E, E_TURN):
                    gather(s)
                if s := stage(h, k, 1, E, E_TURN):
                    scatter(s)

            for b in range(2):
                pool.wait_ge(xr_stored[b], 16 * (B // 2))
            gather((0, 0, 0))
            gather((1, 0, 1))
            pipeline(pool, experts, E + 1, E_LO, E_HI, E_TURN)

            def last(h, k):
                if s := stage(h, k, 0, NG):
                    g, _, kk = s
                    pool.wait_ge(fin_var, g + 1)
                    need(pool, fin_normed, 4 * (g - 1))
                    nc.gpsimd.tensor_tensor(rstd[:, kk, :], veps[:, kk, :], neg_half[:, :],
                                            ALU.pow).then_inc(fin_pow, 1)
                if s := stage(h, k, 1, NG):
                    g = s[0]
                    pool.wait_ge(fin_normed, 4 * g + 2)
                    t = ds(4 * g, 2)
                    nc.gpsimd.tensor_tensor(x_sb[:, t, :], x_sb[:, t, :], acc_sb[:, t, :],
                                            ALU.add).then_inc(fin_ready_pool, 1)

            pipeline(pool, last, NG + 1, 2, NG)

        @block.tensor
        def _(pe):
            pe.wait_ge(consts_ready, 1)
            def prepare(part):
                if part == 0:
                    pe.wait_ge(attn_loaded, 16 * 2)
                    nc.tensor.matmul(bank[3][:, 0:384], ident[:, :], wa[:, :], start=True, stop=False)
                    nc.tensor.matmul(bank[3][:, 0:384], aat[:, :], ab[:, :], start=False, stop=True).then_inc(prep_pe, 1)
                    nc.tensor.matmul(bank[4][:, 0:D], ident[:, :], wp[:, :], start=True, stop=False)
                    nc.tensor.matmul(bank[4][:, 0:D], pat[:, :], pb[:, :], start=False, stop=True).then_inc(prep_pe, 1)
                elif part == 1:
                    pe.wait_ge(prep_act, 2)
                    for j in range(3):
                        last = nc.tensor.transpose(bank[5][:, j * P:(j + 1) * P], wm_raw[:, j * D:(j + 1) * D],
                                                   ident[:, :])
                    last.then_inc(prep_pe, 1)
                    nc.tensor.transpose(bank[6][:, 0:P], wmp[:, :], ident[:, :]).then_inc(prep_pe, 1)
                else:
                    pe.wait_ge(prep_act, 4)
                    for j in range(3):
                        last = nc.tensor.transpose(bank[3][:, j * P:(j + 1) * P], wmT[:, j * D:(j + 1) * D],
                                                   ident[:, :])
                    last.then_inc(prep_pe, 1)
                    nc.tensor.matmul(bank[4][:, 0:D], wp[:, :], wmpT[:, :], start=True, stop=True).then_inc(prep_pe, 1)

            def turn(h, k):
                if s := stage(h, k, 0, NG):
                    g = s[0]
                    pe.wait_ge(ln1_done, 2 * g + 2)
                    pe.wait_ge(ln1_done_act, 2 * g + 2)
                    need(pe, xT_ready, g - 1)
                    for j in range(4):
                        last = nc.tensor.transpose(bank[k][:, j * P:(j + 1) * P], xn[:, k, j, 0:D], ident[:, :])
                    last.then_inc(ln1_turned, 1)
                    first = isinstance(g, int) and g == 0
                    final = isinstance(g, int) and g == NG - 1
                    for j in range(4):
                        last = nc.tensor.matmul(bank[2][:, 0:D + 1], xn[:, k, j, 0:D], xn[:, k, j, :],
                                                start=first and j == 0, stop=final and j == 3)
                    last.then_inc(ln1_used, 1)
                    if isinstance(g, int) and g < 2:
                        prepare(g + 1)

            prepare(0)
            pipeline(pe, turn, NG, 2, NG - 2)

            pe.wait_ge(fold_dve, 1)
            nc.tensor.matmul(bank[3][:, 0:384], gram[:, 0:D], wmT[:, :], start=True, stop=True).then_inc(fold_pe, 1)
            for j in range(3):
                last = nc.tensor.matmul(bank[4][:, j:j + 1], wmT[:, j * D:(j + 1) * D], gram[:, D:D + 1],
                                        start=True, stop=True)
            last.then_inc(fold_pe, 1)
            pe.wait_ge(fold_dve, 2)
            for j in range(3):
                last = nc.tensor.matmul(bank[5][:, j:j + 1], wgram[:, j * D:(j + 1) * D], ones[:, 0:1],
                                        start=True, stop=True)
            last.then_inc(fold_pe, 1)
            pe.wait_ge(fold_dve, 10)
            nc.tensor.matmul(bank[3][:, 0:D], wns[:, 0, :], wns[:, 1, :], start=True, stop=True).then_inc(fold_pe, 1)
            pe.wait_ge(fold_dve, 13)
            nc.tensor.matmul(bank[4][:, 0:1], wns[:, 1, :], bn[:, 7, 0:1], start=True, stop=True).then_inc(fold_pe, 1)
            pe.wait_ge(fold_mean, 2)
            nc.tensor.matmul(bank[5][:, 0:D], wns[:, 2, :], p2T[:, :], start=True, stop=True).then_inc(fold_pe, 1)
            pe.wait_ge(fold_dve, 14)
            nc.tensor.matmul(bank[6][:, 0:D], bv_wide[:, :], p2T[:, :], start=True, stop=True).then_inc(fold_pe, 1)

            pe.wait_ge(xT_ready, NG)
            pe.wait_ge(ffn_loaded, 16)

            def body(h, k):
                s0, s1, s2 = stage(h, k, 0, B), stage(h, k, 1, B), stage(h, k, 2, B)
                if s0:
                    n, _, kk = s0
                    sp_bank = bank[1 + kk]
                    need(pe, exp_done, 2 * (n - 1))
                    nc.tensor.matmul(sp_bank[:, 0:384], ident16[:, :], causal[:, :], start=True, stop=False)
                    pe.wait_ge(z_copied, n + 1)
                    nc.tensor.matmul(sp_bank[:, 0:P], zT[:, kk, 0:P], xT[:, ds(256 * n, P)], start=False, stop=False)
                    nc.tensor.matmul(sp_bank[:, P:384], zT[:, kk, P:256], xT[:, ds(256 * n, 256)],
                                     start=False, stop=True).then_inc(scores_done, 1)
                if s2:
                    n, _, kk = s2
                    pe.wait_ge(probsT_ready, n + 1)
                    pe.wait_ge(vals_copied, n + 1)
                    need(pe, f_ready, 2 * n)
                    nc.tensor.matmul(bank[5][:, 0:P], probsT[:, kk, 0:P], vals[:, kk, 0:P], start=True, stop=True)
                    nc.tensor.matmul(bank[5][:, P:256], probsT[:, kk, P:256], vals[:, kk, 0:P],
                                     start=True, stop=False)
                    nc.tensor.matmul(bank[5][:, P:256], probsT[:, kk, 256:384], vals[:, kk, P:256],
                                     start=False, stop=True).then_inc(f_done, 1)
                if s1:
                    n, _, kk = s1
                    pe.wait_ge(exp_done, 2 * n + 2)
                    need(pe, probsT_ready, n)
                    for j in range(3):
                        last = nc.tensor.transpose(bank[3][:, j * P:(j + 1) * P], probs[:, kk, j * P:(j + 1) * P],
                                                   ident[:, :])
                    last.then_inc(probs_turned, 1)
                if s := stage(h, k, -1, B):
                    turn_queries(s[0])
                if s := stage(h, k, 5, B):
                    n, _, kk = s
                    pe.wait_ge(xr_ready, n + 1)
                    need(pe, xrT_ready, n)
                    for j in range(2):
                        last = nc.tensor.transpose(bank[6][:, j * P:(j + 1) * P], xr[:, kk, j, :], ident[:, :])
                    last.then_inc(xr_turned, 1)
                if s0:
                    n, hh, kk = s0
                    pe.wait_ge(xT_now_loaded[kk], 16 * (hh + 1))
                    need(pe, vals_copied, n)
                    for j in range(2):
                        last = nc.tensor.matmul(bank[4][:, j * P:(j + 1) * P], xT_now[:, kk, j * P:(j + 1) * P],
                                                outw[:, 0, :], start=True, stop=True)
                    last.then_inc(vals_done, 1)
                if s := stage(h, k, 5, B):
                    n, _, kk = s
                    pe.wait_ge(xrT_ready, n + 1)
                    for j in range(2):
                        last = nc.tensor.matmul(bank[7][:, ds(2 * E * n + E * j, E)], xrT[:, kk, j * P:(j + 1) * P],
                                                gate[:, :], start=True, stop=True)
                    last.then_inc(logits_done, 1)

            def turn_queries(n):
                need(pe, z_copied, n)
                nc.tensor.matmul(bank[0][:, 0:256], mix[:, :], xT[:, ds(256 * n, 256)],
                                 start=True, stop=True).then_inc(z_done, 1)

            pe.wait_ge(fold_dve, 15)
            turn_queries(0)
            pe.wait_ge(fold_dve, 18)
            pipeline(pe, body, A_STEPS, A_LO, A_HI)

            pe.wait_ge(soft_dve, 5)
            for a in range(4):
                last = nc.tensor.transpose(bank[0][:, a * P:(a + 1) * P],
                                           score[:, 8 * a:8 * a + 8, :].rearrange("p t e -> p (t e)"), ident[:, :])
            last.then_inc(score_turned, 1)
            for b in range(2):
                pe.wait_ge(xrT_kept[b], 16 * (B // 2))
            pe.wait_ge(consts_ready, 2)

            def shared(h, k):
                s0, s1 = stage(h, k, 0, NG), stage(h, k, 1, NG)

                def out_half(a):
                    if s1:
                        g, _, kk = s1
                        if a == 0:
                            pe.wait_ge(sh_hid, SC * (g + 1))
                            need(pe, sh_out_copied, g)
                        for j in range(2 * a, 2 * a + 2):
                            for c in range(SC):
                                last = nc.tensor.matmul(bank[5][:, j * D:(j + 1) * D],
                                                        shid[:, kk, c, j * P:(j + 1) * P], sd[:, c, :],
                                                        start=c == 0, stop=c == SC - 1)
                        if a == 1:
                            last.then_inc(sh_out_done, 1)

                def sum_counts(c):
                    if s0 and not (isinstance(s0[0], int) and SC * s0[0] + c >= DIGITS):
                        pe.wait_ge(counted, SC * s0[0] + c + 1)
                        nc.tensor.matmul(bank[6][:, 0:7], same_expert[:, :], count[:, :],
                                         start=True, stop=True).then_inc(counts_summed, 1)

                for c in range(SC):
                    if s0 and isinstance(s0[0], int) and SC * s0[0] + c == DIGITS:
                        pe.wait_ge(rank_dve, 1)
                        nc.tensor.transpose(bank[0][:, 0:E], least_wide[0:E, :], ident[0:E, 0:E]).then_inc(rank_pe, 1)
                    if s0:
                        g = s0[0]
                        cols = ds(512 * g, 512)
                        need(pe, sh_gelu, SC * (g - 1) + c + 1)
                        nc.tensor.matmul(bank[1 + c][:, :], sg[:, c * P:(c + 1) * P], xT[:, cols],
                                         start=True, stop=True).then_inc(sh_gate_done, 1)
                        need(pe, sh_up, SC * (g - 1) + c + 1)
                        nc.tensor.matmul(bank[3 + c][:, :], su[:, c * P:(c + 1) * P], xT[:, cols],
                                         start=True, stop=True).then_inc(sh_up_done, 1)
                    sum_counts(c)
                    out_half(c)

            pipeline(pe, shared, NG, 4, NG - 2)

            pe.wait_ge(rank_dve, 6)
            for i, a in enumerate((above_sum, equal_sum)):
                nc.tensor.matmul(bank[7][:, i * E:(i + 1) * E], before[:, :], a[:, :, 31], start=True, stop=True)
            nc.tensor.matmul(bank[7][:, 2 * E:3 * E], ones16[:, :], above_sum[:, :, 31],
                             start=True, stop=True).then_inc(rank_pe, 1)
            pe.wait_ge(rank_dve, 11)
            base_wide = chunk_base[:, :].unsqueeze(2).to_broadcast([P, E, 32])
            for i, a in enumerate((above_sum[:, :, :], equal_taken[:, :, :], base_wide)):
                last = nc.tensor.matmul(bank[0][:, :].rearrange("p (e j) -> p e j", j=32), differ[:, :], a,
                                        start=i == 0, stop=i == 2)
            last.then_inc(rank_pe, 1)
            for i, a in enumerate((above_sum[:, :, 31], equal_taken[:, :, 31], chunk_base[:, :])):
                last = nc.tensor.matmul(bank[6][:, 0:E], shift[:, :], a, start=i == 0, stop=i == 2)
            last.then_inc(rank_pe, 1)
            pe.wait_ge(rank_dve, 12)
            pe.wait_ge(rank_act, 1)

            def look_up(s):
                n, _, k = s
                pe.wait_ge(started_ready, n + 1)
                need(pe, idx_step, PER_IDX * n)
                for t in range(NS):
                    last = nc.tensor.matmul(bank[0][:, t * 33:t * 33 + 33], started[:, k % 2, t * P:(t + 1) * P],
                                            rank_steps[:, ds(n, 1), :].rearrange("p a j -> p (a j)"),
                                            start=True, stop=True)
                last.then_inc(looked_up, 1)

            def turn_tokens(s):
                n, h, k = s
                pe.wait_ge(gathered[k % 2], 16 * NS * (2 * h + k // 2 + 1))
                need(pe, xgT_lo_ready, n)
                for t in range(NS):
                    last = nc.tensor.transpose(bank[1][:, t * P:(t + 1) * P], xg[:, k % 2, t, 0:D], ident[:, :])
                last.then_inc(xg_turned, 1)

            def product(dst, k, c):
                cols = slice(c * P, (c + 1) * P)
                nc.tensor.matmul(dst, w_gu_hi[:, k, cols], xgT_hi[:, k, :], start=True, stop=False)
                nc.tensor.matmul(dst, w_gu_hi[:, k, cols], xgT_lo[:, k, :], start=False, stop=False)
                return nc.tensor.matmul(dst, w_gu_lo[:, k, cols], xgT_hi[:, k, :], start=False, stop=True)

            def gate_up(s, c):
                n, _, k = s
                if c == 0:
                    pe.wait_ge(gu_lo_ready, n + 1)
                    pe.wait_ge(gu_hi_ready, n + 1)
                    pe.wait_ge(xgT_hi_ready, n + 1)
                    pe.wait_ge(xgT_lo_ready, n + 1)
                need(pe, gelu_done, IC * n + c - 1)
                product(bank[2 + c % 2][:, :], k % 2, c).then_inc(gate_done, 1)
                need(pe, hid_done, IC * n + c - 1)
                product(bank[4 + c % 2][:, :], k % 2, IC + c).then_inc(up_done, 1)

            def down(s):
                n, h, k4 = s
                k = k4 % 2
                pe.wait_ge(down_loaded[k], 16 * (2 * h + k4 // 2 + 1))
                pe.wait_ge(hid_done, IC * (n + 1))
                need(pe, eo_scaled, 2 * (n - 1))
                for t in range(NS):
                    tail = isinstance(n, int) and n == E - 1
                    made = bank[2 + t][:, 0:D] if tail else bank[6 + k][:, t * D:(t + 1) * D]
                    for c in range(IC):
                        last = nc.tensor.matmul(made, hid[:, k, c, t * P:(t + 1) * P],
                                                w_down[:, k, c * P:(c + 1) * P], start=c == 0, stop=c == IC - 1)
                    if tail:
                        last.then_inc(tail_done, 1)
                if not tail:
                    last.then_inc(eo_done, 1)

            def experts(h, k):
                this = stage(h, k, 0, E, E_TURN)
                if this:
                    gate_up(this, 0)
                if s := stage(h, k, 1, E, E_TURN):
                    down(s)
                if this:
                    gate_up(this, 1)
                if s := stage(h, k, -1, E, E_TURN):
                    turn_tokens(s)
                if this:
                    gate_up(this, 2)
                if s := stage(h, k, -3, E, E_TURN):
                    look_up(s)
                if this:
                    gate_up(this, 3)

            look_up((0, 0, 0))
            shared(NG // 2, 0)
            for n in range(1, 3):
                look_up((n, 0, n))
            turn_tokens((0, 0, 0))
            pipeline(pe, experts, E + 1, E_LO, E_HI, E_TURN)

        @block.scalar
        def _(act):
            act.dma_start(low_rank[:, :], low_rank_in).then_inc(attn_loaded, 16)
            act.dma_start(attn_w[:, :], attn_w_in).then_inc(attn_loaded, 16)
            act.dma_start(ffn_w[:, :], ffn_w_in).then_inc(ffn_loaded, 16)

            def prepare(part):
                if part == 0:
                    act.wait_ge(prep_pe, 2)
                    nc.scalar.activation(wm_raw[:, :], bank[3][:, 0:384], ACT.Copy).then_inc(prep_act, 1)
                    nc.scalar.activation(wmp[:, :], bank[4][:, 0:D], ACT.Copy).then_inc(prep_act, 1)
                elif part == 1:
                    act.wait_ge(prep_pe, 4)
                    nc.scalar.activation(wmT[:, :].rearrange("p (r k) -> p k r", k=3),
                                         bank[5][:, 0:384].rearrange("p (k r) -> p k r", k=3),
                                         ACT.Copy).then_inc(prep_act, 1)
                    nc.scalar.activation(wmpT[:, :], bank[6][:, 0:P], ACT.Copy).then_inc(prep_act, 1)
                else:
                    act.wait_ge(prep_pe, 6)
                    nc.scalar.activation(wn[:, :, :], bank[3][:, 0:384].rearrange("p (k r) -> p k r", k=3),
                                         ACT.Copy).then_inc(prep_act, 1)
                    nc.scalar.activation(p2T_raw[:, :], bank[4][:, 0:D], ACT.Copy).then_inc(prep_act, 1)

            def first_norm(h, k):
                if s := stage(h, k, 0, NG):
                    g, _, kk = s
                    act.wait_ge(ln1_shift, g + 1)
                    need(act, ln1_used, g - 1)
                    for i in range(2, 4):
                        nc.scalar.activation(xn[:, kk, i, 0:D], x_sb[:, ds(4 * g + i, 1), :].rearrange("p a d -> p (a d)"),
                                             ACT.Identity, bias=shiftm[:, kk, i:i + 1],
                                             scale=rstd[:, kk, i:i + 1]).then_inc(ln1_done_act, 1)
                    if isinstance(g, int) and g == 0:
                        prepare(0)
                if s := stage(h, k, 1, NG):
                    g, _, kk = s
                    act.wait_ge(ln1_turned, g + 1)
                    nc.scalar.activation(xT[:, ds(512 * g, 512)], bank[kk][:, :], ACT.Copy).then_inc(xT_ready, 1)
                    if isinstance(g, int) and g < 2:
                        prepare(g + 1)

            pipeline(act, first_norm, NG + 1, 4, NG)

            def body(h, k):
                s0 = stage(h, k, 0, B)
                if s := stage(h, k, 1, B):
                    n, _, kk = s
                    act.wait_ge(probs_turned, n + 1)
                    need(act, f_done, n - 1)
                    nc.scalar.activation(probsT[:, kk, :], bank[3][:, 0:384], ACT.Copy).then_inc(probsT_ready, 1)
                if s := stage(h, k, -1, B):
                    copy_queries(s[0], s[2])
                if s := stage(h, k, 5, B):
                    n, hh, kk = s
                    act.wait_ge(xr_turned, n + 1)
                    need(act, logits_done, n - 1)
                    need(act, xrT_kept[kk], 16 * hh)
                    nc.scalar.activation(xrT[:, kk, :], bank[6][:, 0:256], ACT.Copy).then_inc(xrT_ready, 1)
                if s0:
                    n, _, kk = s0
                    act.wait_ge(max_step, PER_MAX * (n + 1))
                    need(act, probs_turned, n - 1)
                    need(act, rsums_done, n - 1)
                    for j, (lo, hi) in enumerate(((0, P), (P, 384))):
                        nc.scalar.activation(probs[:, kk, lo:hi], bank[1 + kk][:, lo:hi], ACT.Exp,
                                             bias=nbias[:, kk, j:j + 1], scale=SCALE,
                                             accum_out=psums[:, kk, j:j + 1]).then_inc(exp_done, 1)
                    act.wait_ge(vals_done, n + 1)
                    need(act, f_done, n - 1)
                    nc.scalar.activation(vals[:, kk, :], bank[4][:, 0:256], ACT.Copy).then_inc(vals_copied, 1)
                if s := stage(h, k, 4, B):
                    n, hh, kk = s
                    act.wait_ge(shift_ready, n + 1)
                    need(act, xr_turned, n - 1)
                    need(act, xr_stored[kk], 16 * hh)
                    for j in range(2):
                        last = nc.scalar.activation(
                            xr[:, kk, j, :], x_sb[:, ds(2 * n + j, 1), :].rearrange("p a d -> p (a d)"),
                            ACT.Identity, bias=shift2[:, kk, j:j + 1], scale=rstd2[:, 1 - kk, 2 + j:3 + j])
                    last.then_inc(xr_ready, 1)

            def copy_queries(n, k):
                act.wait_ge(z_done, n + 1)
                need(act, scores_done, n - 1)
                nc.scalar.activation(zT[:, k, :], bank[0][:, 0:256], ACT.Identity,
                                     bias=mix_bias[:, 0:1]).then_inc(z_copied, 1)

            act.wait_ge(fold_dve, 16)
            copy_queries(0, 0)
            pipeline(act, body, A_STEPS, A_LO, A_HI)

            act.wait_ge(soft_dve, 2)
            nc.scalar.activation(logit[:, :, :], logit[:, :, :], ACT.Exp).then_inc(soft_exp, 1)
            act.wait_ge(score_turned, 1)
            nc.scalar.activation(by_expert[:, :], bank[0][:, :], ACT.Copy).then_inc(by_expert_ready, 1)

            def shared(h, k):
                if s := stage(h, k, 0, NG):
                    g = s[0]
                    for c in range(SC):
                        act.wait_ge(sh_gate_done, SC * g + c + 1)
                        need(act, sh_hid, SC * (g - 1) + c + 1)
                        nc.scalar.activation(sgelu[:, c, :], bank[1 + c][:, :], ACT.Gelu).then_inc(sh_gelu, 1)
                        act.wait_ge(sh_up_done, SC * g + c + 1)
                        nc.scalar.activation(sup[:, c, :], bank[3 + c][:, :], ACT.Copy).then_inc(sh_up, 1)
                if s := stage(h, k, 1, NG):
                    g, hh, kk = s
                    act.wait_ge(sh_out_done, g + 1)
                    need(act, sh_stored[kk], 16 * hh)
                    nc.scalar.activation(sout[:, kk, :, :], bank[5][:, :].rearrange("p (j d) -> p j d", d=D),
                                         ACT.Copy).then_inc(sh_out_copied, 1)

            pipeline(act, shared, NG, 4, NG)

            def weights_hi(s):
                n, h, k4 = s
                k = k4 % 2
                act.wait_ge(gu_loaded[k], 16 * (2 * h + k4 // 2 + 1))
                need(act, up_done, IC * (n - 1))
                nc.scalar.activation(w_gu_hi[:, k, :], w_gu[:, k, :], ACT.Copy, scale=W_UP).then_inc(gu_hi_ready, 1)

            def tokens_hi(s):
                n, _, k = s
                act.wait_ge(xg_turned, n + 1)
                need(act, up_done, IC * (n - 1))
                nc.scalar.activation(xgT_hi[:, k % 2, :], bank[1][:, :], ACT.Copy).then_inc(xgT_hi_ready, 1)

            def experts(h, k):
                this, following = stage(h, k, 0, E, E_TURN), stage(h, k, -1, E, E_TURN)

                def gelus(c):
                    n = this[0]
                    act.wait_ge(gate_done, IC * n + c + 1)
                    need(act, hid_done, IC * n + c - 1)
                    nc.scalar.activation(gelu[:, c % 2, :], bank[2 + c % 2][:, :], ACT.Gelu,
                                         scale=1.0 / W_UP).then_inc(gelu_done, 1)

                gelus(0)
                if following:
                    weights_hi(following)
                gelus(1)
                if following:
                    tokens_hi(following)
                gelus(2)
                gelus(3)

            weights_hi((0, 0, 0))
            act.wait_ge(rank_pe, 3)
            nc.scalar.activation(rank_steps[:, :, 0:32], bank[0][:, :].rearrange("p (e j) -> p e j", j=32),
                                 ACT.Copy).then_inc(rank_act, 1)
            shared(NG // 2, 0)
            tokens_hi((0, 0, 0))
            pipeline(act, experts, E, E_LO, E_HI, E_TURN)

            def last_norm(h, k):
                g, _, kk = stage(h, k, 0, NG)
                act.wait_ge(fin_shift, g + 1)
                for i in range(4):
                    v = acc_sb[:, ds(4 * g + i, 1), :].rearrange("p a d -> p (a d)")
                    nc.scalar.activation(v, v, ACT.Identity, bias=shiftm[:, kk, i:i + 1],
                                         scale=rstd[:, kk, i:i + 1]).then_inc(fin_normed, 1)

            pipeline(act, last_norm, NG, 2, NG)

        @block.vector
        def _(dve):
            nc.vector.memset(xn[:, :, :, D:D + 1], 1.0).then_inc(ln1_step, 1)
            nc.vector.memset(stat2[:, :, :, :], 1.0).then_inc(ln1_step, 1)

            LN1 = 8

            def stats(h, j, k):
                g = 4 * h + j
                dve.wait_ge(x_loaded[j], 16 * (h + 1))
                for i in range(4):
                    nc.vector.bn_stats(stat[:, k, i, :],
                                       x_sb[:, ds(4 * g + i, 1), :].rearrange("p a d -> p (a d)")).then_inc(ln1_step, 1)
                dve.wait_ge(ln1_step, 2 + LN1 * g + 4)
                dve.sem_inc(dve_waited, 1)
                for i in range(4):
                    nc.vector.bn_aggr(mv[:, k, i, :], stat[:, k, i, :]).then_inc(ln1_step, 1)
                dve.wait_ge(ln1_step, 2 + LN1 * (g + 1))
                nc.vector.tensor_scalar(veps[:, k, :], mv[:, k, :, 1], EPS, None, ALU.add).then_inc(ln1_var, 1)

            def norm(g, k):
                dve.wait_ge(ln1_rstd, g + 1)
                need(dve, ln1_done_act, 2 * (g - 1))
                nc.vector.scalar_tensor_tensor(out=shiftm[:, k, :], in0=mv[:, k, :, 0], scalar=-1.0, in1=rstd[:, k, :],
                                               op0=ALU.mult, op1=ALU.mult).then_inc(ln1_shift, 1)
                need(dve, ln1_used, g - 1)
                for i in range(2):
                    nc.vector.tensor_scalar(xn[:, k, i, 0:D],
                                            x_sb[:, ds(4 * g + i, 1), :].rearrange("p a d -> p (a d)"),
                                            mv[:, k, i, 0:1], rstd[:, k, i:i + 1], ALU.subtract,
                                            ALU.mult).then_inc(ln1_done, 1)

            stats(0, 0, 0)
            for g in range(1, 4):
                stats(0, g, g % 2)
                norm(g - 1, (g - 1) % 2)
            with dve.Fori(1, NG // 4) as h:
                for j in range(4):
                    stats(h, j, j % 2)
                    norm(4 * h + j - 1, (j - 1) % 2)
            dve.wait_ge(prep_act, 6)
            nc.vector.tensor_reduce(p2T_mean[:, :], p2T_raw[:, :], AX, ALU.add).then_inc(fold_mean, 1)
            dve.wait_ge(fold_mean, 1)
            nc.vector.scalar_tensor_tensor(out=p2T[:, :], in0=p2T_mean[:, :].to_broadcast([P, D]), scalar=-1.0 / D,
                                           in1=p2T_raw[:, :], op0=ALU.mult, op1=ALU.add).then_inc(fold_mean, 1)
            norm(NG - 1, (NG - 1) % 2)

            dve.wait_ge(ln1_used, NG)
            nc.vector.tensor_scalar(gram[:, :], bank[2][:, 0:D + 1], 1.0 / TOK, None, ALU.mult).then_inc(fold_dve, 1)
            dve.wait_ge(fold_pe, 2)
            dve.wait_ge(prep_act, 6)
            nc.vector.tensor_tensor(wgram[:, :], bank[3][:, 0:384], wmT[:, :], ALU.mult).then_inc(fold_dve, 1)
            nc.vector.tensor_copy(bn[:, 0, :], bank[4][:, 0:3]).then_inc(fold_dve, 1)
            dve.wait_ge(fold_dve, 3)
            nc.vector.tensor_tensor(bn[:, 1, :], bn[:, 0, :], bn[:, 0, :], ALU.mult).then_inc(fold_dve, 1)
            dve.wait_ge(fold_pe, 3)
            dve.wait_ge(fold_dve, 4)
            nc.vector.tensor_tensor(bn[:, 3, :], bank[5][:, 0:3], bn[:, 1, :], ALU.subtract).then_inc(fold_dve, 1)
            dve.wait_ge(fold_dve, 5)
            nc.vector.tensor_scalar(bn[:, 2, :], bn[:, 3, :], 0.0, None, ALU.max).then_inc(fold_dve, 1)
            dve.wait_ge(fold_dve, 6)
            nc.vector.tensor_scalar(bn[:, 4, :], bn[:, 2, :], EPS, None, ALU.add).then_inc(fold_dve, 1)
            dve.wait_ge(fold_pow, 1)
            nc.vector.tensor_tensor(bn[:, 6, :], bn[:, 5, :], gamma[:, :], ALU.mult).then_inc(fold_dve, 1)
            dve.wait_ge(fold_dve, 8)
            for j in range(2):
                nc.vector.tensor_scalar(wns[:, j, :], wn[:, j, :], bn[:, 6, j:j + 1], None, ALU.mult).then_inc(fold_dve, 1)
            nc.vector.tensor_tensor(bn[:, 1, :], bn[:, 0, :], bn[:, 6, :], ALU.mult).then_inc(fold_dve, 1)
            nc.vector.tensor_scalar(wns[:, 2, :], wn[:, 2, :], bn[:, 6, 2:3], None, ALU.mult).then_inc(fold_dve, 1)
            dve.wait_ge(fold_dve, 11)
            nc.vector.tensor_tensor(bn[:, 7, :], beta[:, :], bn[:, 1, :], ALU.subtract).then_inc(fold_dve, 1)
            dve.wait_ge(fold_dve, 13)
            nc.vector.tensor_copy(bv_wide[:, :], bn[:, 7, 2:3].to_broadcast([P, P])).then_inc(fold_dve, 1)
            dve.wait_ge(fold_pe, 4)
            nc.vector.tensor_copy(mix[:, :], bank[3][:, 0:D]).then_inc(fold_dve, 1)
            dve.wait_ge(fold_pe, 5)
            nc.vector.tensor_copy(mix_bias[:, :], bank[4][:, 0:1]).then_inc(fold_dve, 1)
            dve.wait_ge(fold_pe, 6)
            nc.vector.tensor_copy(outw[:, 0, :], bank[5][:, 0:D]).then_inc(fold_dve, 1)
            dve.wait_ge(fold_pe, 7)
            nc.vector.tensor_copy(outw[:, 1, :], bank[6][:, 0:D]).then_inc(fold_dve, 1)
            dve.wait_ge(fold_dve, 18)

            def body(h, k):
                if s := stage(h, k, 1, B):
                    n, _, kk = s
                    dve.wait_ge(exp_done, 2 * n + 2)
                    need(dve, f_ready, 2 * (n - 1))
                    nc.vector.reciprocal(rsums[:, kk, :], psums[:, kk, :]).then_inc(rsums_done, 1)
                if s := stage(h, k, 0, B):
                    n, _, kk = s
                    dve.wait_ge(scores_done, n + 1)
                    for j, (lo, hi) in enumerate(((0, P), (P, 384))):
                        nc.vector.tensor_reduce(top[:, kk, j:j + 1], bank[1 + kk][:, lo:hi], AX,
                                                ALU.max).then_inc(max_step, 1)
                    dve.wait_ge(max_step, PER_MAX * n + 2)
                    nc.vector.tensor_scalar(nbias[:, kk, :], top[:, kk, :], -SCALE, None, ALU.mult).then_inc(max_step, 1)
                if s := stage(h, k, 2, B):
                    n, _, kk = s
                    dve.wait_ge(f_done, n + 1)
                    dve.wait_ge(rsums_done, n + 1)
                    for j in range(2):
                        nc.vector.scalar_tensor_tensor(
                            out=f[:, kk, j, :], in0=bank[5][:, j * D:(j + 1) * D], scalar=rsums[:, kk, j:j + 1],
                            in1=outw[:, 1, :], op0=ALU.mult, op1=ALU.add).then_inc(f_ready, 1)
                    for j in range(2):
                        dve.wait_ge(f_ready, 2 * n + 1 + j)
                        nc.vector.bn_stats(stat2[:, kk, j, :], f[:, kk, j, :]).then_inc(f_stats, 1)
                if s := stage(h, k, 4, B):
                    n, _, kk = s
                    dve.wait_ge(norm_pow, n + 2)
                    need(dve, xr_ready, n - 1)
                    nc.vector.scalar_tensor_tensor(out=shift2[:, kk, :], in0=mv2[:, 1 - kk, 2:4, 0], scalar=-1.0,
                                                   in1=rstd2[:, 1 - kk, 2:4], op0=ALU.mult,
                                                   op1=ALU.mult).then_inc(shift_ready, 1)
                if s := stage(h, k, 3, B):
                    n, _, kk = s
                    dve.wait_ge(norm_pow, n + 1)
                    for j in range(2):
                        xt = x_sb[:, ds(2 * n + j, 1), :].rearrange("p a d -> p (a d)")
                        nc.vector.scalar_tensor_tensor(out=xt, in0=f[:, kk, j, :], scalar=rstd2[:, kk, j:j + 1],
                                                       in1=xt, op0=ALU.mult, op1=ALU.add).then_inc(x2_ready, 1)
                    for j in range(2):
                        dve.wait_ge(x2_ready, 2 * n + 1 + j)
                        dve.sem_inc(dve_waited, 1)
                        nc.vector.bn_stats(stat2[:, 1 - kk, 2 + j, :],
                                           x_sb[:, ds(2 * n + j, 1), :].rearrange("p a d -> p (a d)")).then_inc(x2_stats, 1)
                if s := stage(h, k, 2, B + 2):
                    n, _, kk = s
                    if not isinstance(n, int) or n < B:
                        dve.wait_ge(f_stats, 2 * n + 2)
                    if not isinstance(n, int) or 0 < n <= B:
                        dve.wait_ge(x2_stats, 2 * n)
                    dve.sem_inc(dve_waited, 1)
                    for j in range(4):
                        nc.vector.bn_aggr(mv2[:, kk, j, :], stat2[:, kk, j, :]).then_inc(norm_aggr, 1)
                    dve.wait_ge(norm_aggr, 4 * n + 4)
                    nc.vector.tensor_scalar(veps2[:, kk, :], mv2[:, kk, :, 1], EPS, None, ALU.add).then_inc(norm_var, 1)

            pipeline(dve, body, A_STEPS, A_LO, A_HI)

            dve.wait_ge(logits_done, B)
            lg = bank[7][:, :].rearrange("p (t e) -> p t e", e=E)
            nc.vector.tensor_reduce(rmax[:, :], lg, AX, ALU.max).then_inc(soft_dve, 1)
            dve.wait_ge(soft_dve, 1)
            nc.vector.tensor_tensor(logit[:, :, :], lg, rmax[:, :].unsqueeze(2).to_broadcast([P, NT, E]),
                                    ALU.subtract).then_inc(soft_dve, 1)
            dve.wait_ge(soft_exp, 1)
            nc.vector.tensor_reduce(rsum[:, :], logit[:, :, :], AX, ALU.add).then_inc(soft_dve, 1)
            dve.wait_ge(soft_dve, 3)
            nc.vector.reciprocal(rinv[:, :], rsum[:, :]).then_inc(soft_dve, 1)
            dve.wait_ge(soft_dve, 4)
            nc.vector.tensor_tensor(score[:, :, :], logit[:, :, :], rinv[:, :].unsqueeze(2).to_broadcast([P, NT, E]),
                                    ALU.mult).then_inc(soft_dve, 1)

            dve.wait_ge(consts_ready, 2)
            nc.vector.tensor_scalar(digit_clamped[:, :, :], digit_shift[:, :, :], 0.0, None, ALU.max).then_inc(search_step, 1)
            dve.wait_ge(search_step, 1)
            nc.vector.tensor_tensor(digit_bits[:, :, :], digits[:, :, :], digit_clamped[:, :, :],
                                    ALU.logical_shift_left).then_inc(search_step, 1)
            dve.wait_ge(search_step, 2)
            nc.vector.memset(digit_bits[:, DIGITS:, :], 0).then_inc(search_step, 1)
            nc.vector.tensor_copy(cand[:, 0, :], digit_bits[:, 0, :]).then_inc(search_step, 1)
            nc.vector.memset(count[:, 3:7], float(CAP)).then_inc(search_step, 1)
            for side, digits_there, op in ((0, slice(0, LEFT), ALU.logical_shift_left),
                                           (1, slice(LEFT, DIGITS), ALU.logical_shift_right)):
                nc.vector.tensor_tensor(four_bits[:, digits_there, :], four[:, digits_there, :].bitcast(I32),
                                        place_shift[:, side, digits_there, :], op).then_inc(search_step, 1)
            dve.wait_ge(search_step, 3)
            nc.vector.tensor_tensor(digit_flip[:, :, :], digit_bits[:, 0:DIGITS, :], digit_bits[:, 1:, :],
                                    ALU.bitwise_xor).then_inc(search_step, 1)
            dve.wait_ge(search_step, 8)
            nc.vector.tensor_tensor(digit_flip[:, :, :], digit_flip[:, :, :], four_bits[:, :, :],
                                    ALU.bitwise_xor).then_inc(search_step, 1)
            dve.wait_ge(by_expert_ready, 1)
            FIRST, PER = 9, 3

            def search(i, k, side):
                dve.wait_ge(search_step, FIRST + PER * i)
                for j in range(3):
                    last = nc.vector.tensor_scalar(hits[:, j, :], by_expert[:, :], cand[:, k, j:j + 1].bitcast(F32), None,
                                                   ALU.is_ge, ALU.add, accum_out=count[:, j:j + 1])
                last.then_inc(counted, 1)
                nc.vector.tensor_tensor(cand_next[:, :], cand[:, k, :],
                                        digit_flip[:, ds(i, 1), :].rearrange("p a j -> p (a j)"),
                                        ALU.bitwise_xor).then_inc(search_step, 1)
                dve.wait_ge(counts_summed, i + 1)
                nc.vector.tensor_scalar(enough[:, :], bank[6][:, 0:7], float(CAP), None,
                                        ALU.is_ge, ALU.add, accum_out=four_plus_digit[:, :]).then_inc(search_step, 1)
                dve.wait_ge(search_step, FIRST + PER * i + 2)
                nc.vector.scalar_tensor_tensor(out=cand[:, 1 - k, :], in0=four_plus_digit[:, :].bitcast(I32).to_broadcast([P, 3]),
                                               scalar=place_shift[:, side, ds(i, 1), 0], in1=cand_next[:, :],
                                               op0=(ALU.logical_shift_left, ALU.logical_shift_right)[side],
                                               op1=ALU.bitwise_xor).then_inc(search_step, 1)

            for i in range(LEFT):
                search(i, i % 2, 0)
            with dve.Fori(LEFT // 2, DIGITS // 2) as h:
                for k in range(2):
                    search(2 * h + k, k, 1)
            search(DIGITS - 1, 0, 1)
            dve.wait_ge(search_step, FIRST + PER * DIGITS)

            def ranks():
                nc.vector.tensor_copy(least_wide[0:E, :],
                                      cand[0:E, 1, 0:1].bitcast(F32).to_broadcast([E, P])).then_inc(rank_dve, 1)
                dve.wait_ge(rank_pe, 1)
                nc.vector.tensor_copy(least[:, :], bank[0][:, 0:E]).then_inc(rank_dve, 1)
                dve.wait_ge(rank_dve, 2)
                dve.wait_ge(chunks_loaded, 16)
                ch = chunked[:, :, :].rearrange("p j e -> p e j")
                lw = least[:, :].unsqueeze(2).to_broadcast([P, E, 32])
                nc.vector.tensor_tensor(above[:, :, :], ch, lw, ALU.is_gt).then_inc(rank_dve, 1)
                nc.vector.tensor_tensor(equal[:, :, :], ch, lw, ALU.is_equal).then_inc(rank_dve, 1)

                def flat(a):
                    return a[:, :, :].rearrange("p e j -> p (e j)")

                for i, (src, dst) in enumerate(((above, above_sum), (equal, equal_sum))):
                    dve.wait_ge(rank_dve, 3 + i)
                    nc.vector.tensor_tensor_scan(flat(dst), flat(scan_keep), flat(src), 0.0,
                                                 ALU.mult, ALU.add).then_inc(rank_dve, 1)
                dve.wait_ge(rank_pe, 2)
                nc.vector.tensor_scalar(wanted[:, :], bank[7][:, 2 * E:3 * E], -1.0, float(CAP), ALU.mult,
                                        ALU.add).then_inc(rank_dve, 1)
                dve.wait_ge(rank_dve, 7)
                nc.vector.tensor_tensor(equal_before[:, :], bank[7][:, E:2 * E], wanted[:, :], ALU.min).then_inc(rank_dve, 1)
                dve.wait_ge(rank_dve, 8)
                nc.vector.tensor_tensor(wanted_here[:, :], wanted[:, :], equal_before[:, :],
                                        ALU.subtract).then_inc(rank_dve, 1)
                nc.vector.tensor_tensor(chunk_base[:, :], bank[7][:, 0:E], equal_before[:, :], ALU.add).then_inc(rank_dve, 1)
                dve.wait_ge(rank_dve, 9)
                nc.vector.tensor_tensor(equal_taken[:, :, :], equal_sum[:, :, :],
                                        wanted_here[:, :].unsqueeze(2).to_broadcast([P, E, 32]),
                                        ALU.min).then_inc(rank_dve, 1)
                dve.wait_ge(rank_pe, 4)
                nc.vector.tensor_copy(first_rank[:, :], bank[6][:, 0:E]).then_inc(rank_dve, 1)
                dve.wait_ge(rank_dve, 12)

            ranks()

            def start_slots(s):
                n, _, k = s
                need(dve, looked_up, n - 1)
                nc.vector.tensor_scalar(started[:, k % 2, :], slot_row[:, :], first_rank[:, ds(n, 1)], None,
                                        ALU.is_ge).then_inc(started_ready, 1)

            def index(s):
                n, h, k4 = s
                dve.wait_ge(looked_up, n + 1)
                lk = bank[0][:, 0:NS * 33].rearrange("p (t j) -> p t j", j=33)
                nc.vector.tensor_tensor(passed[:, :, :], lk[:, :, 0:32], slot_col[:, :, :], ALU.is_le).then_inc(idx_step, 1)
                dve.wait_ge(idx_step, PER_IDX * n + 1)
                nc.vector.tensor_reduce(passed_sum[:, :], passed[:, :, :], AX, ALU.add).then_inc(idx_step, 1)
                dve.wait_ge(idx_step, PER_IDX * n + 2)
                nc.vector.scalar_tensor_tensor(out=idx_f[:, :], in0=lk[:, :, 32], scalar=32.0, in1=passed_sum[:, :],
                                               op0=ALU.mult, op1=ALU.add).then_inc(idx_step, 1)
                dve.wait_ge(idx_step, PER_IDX * n + 3)
                nc.vector.tensor_scalar(idx_in[:, k4, :], idx_f[:, :], -32.0, None, ALU.add).then_inc(idx_step, 1)

            def keep_scores(s):
                n, h, k4 = s
                dve.wait_ge(gathered[k4 % 2], 16 * NS * (2 * h + k4 // 2 + 1))
                need(dve, eo_scaled, 2 * (n - 3))
                nc.vector.tensor_scalar(weight[:, k4, :].unsqueeze(2), xg[:, k4 % 2, :, ds(D + n, 1)], 1.0 / W_UP, None,
                                        ALU.mult).then_inc(kept, 1)

            def weights_lo(s):
                n, _, k4 = s
                k = k4 % 2
                dve.wait_ge(gu_hi_ready, n + 1)
                need(dve, up_done, IC * (n - 1))
                nc.vector.scalar_tensor_tensor(out=w_gu_lo[:, k, :], in0=w_gu[:, k, :], scalar=W_UP,
                                               in1=w_gu_hi[:, k, :], op0=ALU.mult,
                                               op1=ALU.subtract).then_inc(gu_lo_ready, 1)

            def tokens_lo(s):
                n, _, k4 = s
                k = k4 % 2
                dve.wait_ge(xgT_hi_ready, n + 1)
                need(dve, up_done, IC * (n - 1))
                nc.vector.tensor_tensor(xgT_lo[:, k, :], bank[1][:, :], xgT_hi[:, k, :],
                                        ALU.subtract).then_inc(xgT_lo_ready, 1)

            def scale_out(s):
                n, h, k4 = s
                k = k4 % 2
                if isinstance(n, int) and n == E - 1:
                    dve.wait_ge(scattered[k], 16 * NS * (E // 2 - 1))
                    nc.vector.tensor_copy(idx_out[:, k4, :], idx_in[:, k4, :]).then_inc(tail_scaled, 1)
                    for t in range(NS):
                        dve.wait_ge(tail_done, t + 1)
                        dve.wait_ge(kept, E)
                        nc.vector.tensor_scalar(eo[:, k, t, :], bank[2 + t][:, 0:D],
                                                weight[:, k4, t:t + 1], None, ALU.mult).then_inc(tail_scaled, 1)
                    return
                dve.wait_ge(eo_done, n + 1)
                dve.wait_ge(kept, n + 1)
                need(dve, scattered[k], 16 * NS * (2 * h + k4 // 2))
                nc.vector.tensor_copy(idx_out[:, k4, :], idx_in[:, k4, :]).then_inc(eo_scaled, 1)
                nc.vector.tensor_tensor(eo[:, k, :, :], bank[6 + k][:, :].rearrange("p (t d) -> p t d", d=D),
                                        weight[:, k4, :].unsqueeze(2).to_broadcast([P, NS, D]),
                                        ALU.mult).then_inc(eo_scaled, 1)

            def experts(h, k):
                this, following = stage(h, k, 0, E, E_TURN), stage(h, k, -1, E, E_TURN)
                later = stage(h, k, -3, E, E_TURN)

                def hidden(c):
                    if this:
                        n, _, kk = this
                        if c == 0:
                            need(dve, eo_done, n - 1)
                        dve.wait_ge(gelu_done, IC * n + c + 1)
                        dve.wait_ge(up_done, IC * n + c + 1)
                        nc.vector.tensor_tensor(hid[:, kk % 2, c, :], gelu[:, c % 2, :], bank[4 + c % 2][:, :],
                                                ALU.mult).then_inc(hid_done, 1)

                hidden(0)
                if later:
                    start_slots(later)
                if following:
                    weights_lo(following)
                if s := stage(h, k, 1, E, E_TURN):
                    scale_out(s)
                hidden(1)
                if following:
                    tokens_lo(following)
                    keep_scores(following)
                hidden(2)
                hidden(3)
                if later:
                    index(later)

            for n in range(2):
                start_slots((n, 0, n))
            index((0, 0, 0))
            start_slots((2, 0, 2))
            for n in range(1, 3):
                index((n, 0, n))
            weights_lo((0, 0, 0))
            tokens_lo((0, 0, 0))
            keep_scores((0, 0, 0))
            pipeline(dve, experts, E + 1, E_LO, E_HI, E_TURN)

            def last_stats(h, j):
                g = 4 * h + j
                k = j % 2
                dve.wait_ge(sum_loaded[j], 16 * (h + 1))
                for i in range(4):
                    nc.vector.bn_stats(stat[:, k, i, :],
                                       acc_sb[:, ds(4 * g + i, 1), :].rearrange("p a d -> p (a d)")).then_inc(fin_step, 1)
                dve.wait_ge(fin_step, 8 * g + 4)
                dve.sem_inc(dve_waited, 1)
                for i in range(4):
                    nc.vector.bn_aggr(mv[:, k, i, :], stat[:, k, i, :]).then_inc(fin_step, 1)
                dve.wait_ge(fin_step, 8 * (g + 1))
                nc.vector.tensor_scalar(veps[:, k, :], mv[:, k, :, 1], EPS, None, ALU.add).then_inc(fin_var, 1)

            def last_shift(g, k):
                dve.wait_ge(fin_pow, g + 1)
                need(dve, fin_normed, 4 * (g - 1))
                nc.vector.scalar_tensor_tensor(out=shiftm[:, k, :], in0=mv[:, k, :, 0], scalar=-1.0, in1=rstd[:, k, :],
                                               op0=ALU.mult, op1=ALU.mult).then_inc(fin_shift, 1)

            def last_add(g):
                dve.wait_ge(fin_normed, 4 * g + 4)
                t = ds(4 * g + 2, 2)
                nc.vector.tensor_tensor(x_sb[:, t, :], x_sb[:, t, :], acc_sb[:, t, :], ALU.add).then_inc(fin_ready_dve, 1)

            last_stats(0, 0)
            for g in range(1, 4):
                last_stats(0, g)
                last_shift(g - 1, (g - 1) % 2)
                if g >= 2:
                    last_add(g - 2)
            with dve.Fori(1, NG // 4) as h:
                for j in range(4):
                    last_stats(h, j)
                    last_shift(4 * h + j - 1, (j - 1) % 2)
                    last_add(4 * h + j - 2)
            last_shift(NG - 1, (NG - 1) % 2)
            last_add(NG - 2)
            last_add(NG - 1)


def kernel(**inputs):
    import numpy as np
    import concourse.bacc as bacc
    from concourse.bass_utils import run_bass_kernel_spmd

    a = {k: np.asarray(v) for k, v in inputs.items()}
    x = a["L0_attn_x"]
    wg, wu, wd = a["L0_ffn_Wg"], a["L0_ffn_Wu"], a["L0_ffn_Wd"]
    n_exp, hidden, d = wg.shape
    down = wd.transpose(0, 2, 1).reshape(n_exp, hidden // P, P, d).transpose(0, 2, 1, 3).reshape(n_exp, P, hidden)
    shared_down = a["L0_ffn_Sd"].T.reshape(-1, P, d).transpose(1, 0, 2).reshape(P, -1)
    arrays = {
        "x": x.reshape(-1, d),
        "low_rank": np.concatenate([a["L0_attn_lora_attn_A"].T, a["L0_attn_lora_attn_B"], a["L0_attn_lora_proj_A"].T,
                                    a["L0_attn_lora_proj_B"]], axis=1),
        "attn_w": np.concatenate([a["L0_attn_W_attn"].reshape(d, 3 * d), a["L0_attn_W_proj"],
                                  a["L0_attn_bn_gamma"].reshape(3, d).T, a["L0_attn_bn_beta"].reshape(3, d).T], axis=1),
        "ffn_w": np.concatenate([a["L0_ffn_Sg"].T, a["L0_ffn_Su"].T, shared_down, a["L0_ffn_gate_w"].T], axis=1),
        "w_experts": np.concatenate([wg.transpose(0, 2, 1), wu.transpose(0, 2, 1), down], axis=2),
    }
    arrays = {k: np.ascontiguousarray(v) for k, v in arrays.items()}
    nc = bacc.Bacc("TRN2", target_bir_lowering=False, num_devices=1)
    args = {k: nc.dram_tensor(f"in_{k}", v.shape, mybir.dt.from_np(v.dtype), kind="ExternalInput").ap()
            for k, v in arrays.items()}
    out = nc.dram_tensor("out", (x.shape[0] * x.shape[1], d), F32, kind="ExternalOutput").ap()
    build(nc, *args.values(), out)
    r = run_bass_kernel_spmd(nc, [{f"in_{k}": v for k, v in arrays.items()}], core_ids=[0])
    return r.results[0]["out"].reshape(x.shape)
```

```python
from contextlib import ExitStack

import concourse.bass as bass
from concourse import mybir

F32 = mybir.dt.float32
BF16 = mybir.dt.bfloat16
F16 = mybir.dt.float16
I32 = mybir.dt.int32
ALU = mybir.AluOpType
ACT = mybir.ActivationFunctionType
AX = mybir.AxisListType.X

P = 128
EPS = 1e-5
MASKED = -1.0e30
ds = bass.ds


def pipeline(eng, body, steps, lo, hi, turn=2):
    for n in range(lo):
        body(n // turn, n % turn)
    with eng.Fori(lo // turn, hi // turn) as h:
        for k in range(turn):
            body(h, k)
    for n in range(hi, steps):
        body(n // turn, n % turn)


def stage(h, k, behind, count, turn=2):
    n = turn * h + k - behind
    if isinstance(n, int) and not 0 <= n < count:
        return None
    return n, h + (k - behind) // turn, (k - behind) % turn


def need(eng, semaphore, value):
    if not isinstance(value, int) or value > 0:
        eng.wait_ge(semaphore, value)


def build(nc, x, low_rank_in, attn_w_in, ffn_w_in, w_experts, out):
    TOK = x.shape[0]
    D = x.shape[1]
    NT = TOK // P
    B = TOK // 256
    R = low_rank_in.shape[0]
    E = w_experts.shape[0]
    CAP = TOK * 2 // E
    NS = CAP // P
    IC = w_experts.shape[2] // (3 * P)
    GU = 2 * IC * P
    SC = (ffn_w_in.shape[1] - E) // (3 * P)
    NG = TOK // 512
    ROW = D + E
    DIGITS = 15
    FOUR_BIT = 21
    LEFT = (2 * DIGITS - 2 - FOUR_BIT) // 2 + 1
    UPPER = DIGITS - 8
    SCALE = float(D) ** -0.5
    W_UP = 64.0
    assert D == P and CAP == 512 and E * 8 == P and NT * E == 512 and NG * 2 == DIGITS + 1

    table = nc.dram_tensor("token_table", [TOK, ROW], F32, kind="Internal").ap()
    acc = nc.dram_tensor("ffn_sum", [TOK, D], F32, kind="Internal").ap()

    with ExitStack() as ctx:
        def sb(name, shape, dt=F32):
            return ctx.enter_context(nc.sbuf_tensor(name, shape, dt))

        def sem(name):
            return ctx.enter_context(nc.semaphore(name))

        bank = [ctx.enter_context(nc.psum_tensor(f"bank{i}", [P, 512], F32)) for i in range(8)]

        x_sb = sb("x_sb", [P, NT, D])
        xT = sb("xT", [P, TOK])
        ident = sb("ident", [P, P])
        ident16 = sb("ident16", [P, P], BF16)
        causal = sb("causal", [P, 384], BF16)
        ones16 = sb("ones16", [P, P], F16)
        before = sb("before", [P, P], F16)
        differ = sb("differ", [P, P], F16)
        shift = sb("shift", [P, P], F16)
        same_expert = sb("same_expert", [P, P])
        neg_half = sb("neg_half", [P, 4])
        slot_row = sb("slot_row", [P, CAP], F16)
        slot_col = sb("slot_col", [P, NS, 32])
        scan_keep = sb("scan_keep", [P, E, 32])
        digits = sb("digits", [P, DIGITS + 1, 3], I32)
        digit_shift = sb("digit_shift", [P, DIGITS + 1, 3], I32)
        digit_clamped = sb("digit_clamped", [P, DIGITS + 1, 3], I32)
        digit_bits = sb("digit_bits", [P, DIGITS + 1, 3], I32)
        digit_flip = sb("digit_flip", [P, DIGITS, 3], I32)
        place_shift = sb("place_shift", [P, 2, DIGITS, 3], I32)
        four = sb("four", [P, DIGITS, 3])
        four_bits = sb("four_bits", [P, DIGITS, 3], I32)

        low_rank = sb("low_rank", [R, 6 * P])
        aat, ab = low_rank[:, 0:P], low_rank[:, P:4 * P]
        pat, pb = low_rank[:, 4 * P:5 * P], low_rank[:, 5 * P:6 * P]
        attn_w = sb("attn_w", [P, 4 * D + 6])
        wa, wp = attn_w[:, 0:3 * D], attn_w[:, 3 * D:4 * D]
        gamma, beta = attn_w[:, 4 * D:4 * D + 3], attn_w[:, 4 * D + 3:4 * D + 6]
        wm_raw = sb("wm_raw", [P, 3 * D])
        wmT = sb("wmT", [P, 3 * D])
        wn = sb("wn", [P, 3, D])
        wmp = sb("wmp", [P, D])
        wmpT = sb("wmpT", [P, D])
        p2T = sb("p2T", [P, D])
        gram = sb("gram", [P, D + 1])
        wgram = sb("wgram", [P, 3 * D])
        bn = sb("bn", [P, 8, 3])
        wns = sb("wns", [P, 3, D])
        bv_wide = sb("bv_wide", [P, P])
        mix = sb("mix", [P, D])
        mix_bias = sb("mix_bias", [P, 1])
        p2T_raw = sb("p2T_raw", [P, D])
        p2T_mean = sb("p2T_mean", [P, 1])
        outw = sb("outw", [P, 2, D])
        ones = sb("ones", [P, P])

        xn = sb("xn", [P, NG, 4, D + 1])
        stat = sb("stat", [P, 2, 4, 6])
        mv = sb("mv", [P, 2, 4, 2])
        veps = sb("veps", [P, 2, 4])
        rstd = sb("rstd", [P, 2, 4])
        shiftm = sb("shiftm", [P, 2, 4])

        xT_now = sb("xT_now", [P, 2, 256])
        vals = sb("vals", [P, 2, 256])
        zT = sb("zT", [P, 2, 256])
        top = sb("top", [P, 2, 2])
        nbias = sb("nbias", [P, 2, 2])
        probs = sb("probs", [P, 2, 384])
        psums = sb("psums", [P, 2, 2])
        rsums = sb("rsums", [P, 2, 2])
        probsT = sb("probsT", [P, 2, 384])
        f = sb("f", [P, 2, 2, D])
        squares = sb("squares", [P, D])
        square_sum = sb("square_sum", [P, 2, 2])
        stat2 = sb("stat2", [P, 2, 2, 6])
        mv2 = sb("mv2", [P, 2, 2, 2])
        veps2 = sb("veps2", [P, 2, 4])
        rstd2 = sb("rstd2", [P, 2, 4])
        xr = sb("xr", [P, 2, 2, D])
        xrT = sb("xrT", [P, 2, 256])

        ffn_w = sb("ffn_w", [P, 3 * SC * P + E])
        sg, su = ffn_w[:, 0:SC * P], ffn_w[:, SC * P:2 * SC * P]
        sd = ffn_w[:, 2 * SC * P:3 * SC * P].rearrange("p (c d) -> p c d", d=D)
        gate = ffn_w[:, 3 * SC * P:]
        logit = sb("logit", [P, NT, E])
        rmax = sb("rmax", [P, NT])
        rsum = sb("rsum", [P, NT])
        rinv = sb("rinv", [P, NT])
        score = sb("score", [P, NT, E])
        by_expert = sb("by_expert", [P, 512])
        upper = sb("upper", [P, 512], BF16)
        hits = sb("hits", [P, 3, 512], BF16)
        cand = sb("cand", [P, 2, 3], I32)
        cand_next = sb("cand_next", [P, 3], I32)
        enough = sb("enough", [P, 7])
        four_plus_digit = sb("four_plus_digit", [P, 1])
        count = sb("count", [P, 7])
        least_wide = sb("least_wide", [P, P])
        least = sb("least", [P, E])
        chunked = sb("chunked", [P, 32, E])
        above = sb("above", [P, E, 32])
        equal = sb("equal", [P, E, 32])
        above_sum = sb("above_sum", [P, E, 32], F16)
        equal_sum = sb("equal_sum", [P, E, 32], F16)
        equal_taken = sb("equal_taken", [P, E, 32], F16)
        wanted = sb("wanted", [P, E])
        equal_before = sb("equal_before", [P, E])
        wanted_here = sb("wanted_here", [P, E])
        chunk_base = sb("chunk_base", [P, E], F16)
        rank_steps = sb("rank_steps", [P, E, 33], F16)
        first_rank = sb("first_rank", [P, E])
        started = sb("started", [P, 2, CAP], F16)
        passed = sb("passed", [P, NS, 32])
        passed_sum = sb("passed_sum", [P, NS])
        idx_f = sb("idx_f", [P, NS])
        idx_in = sb("idx_in", [P, 4, NS], I32)
        idx_out = sb("idx_out", [P, 4, NS], I32)

        sgelu = sb("sgelu", [P, SC, 512])
        sup = sb("sup", [P, SC, 512])
        shid = sb("shid", [P, 2, SC, 512])
        sout = sb("sout", [P, 2, 4, D])

        w_gu = sb("w_gu", [P, 2, GU])
        w_gu_hi = sb("w_gu_hi", [P, 2, GU], F16)
        w_gu_lo = sb("w_gu_lo", [P, 2, GU], F16)
        w_down = sb("w_down", [P, 2, IC * P])
        xg = sb("xg", [P, 2, NS, ROW])
        weight = sb("weight", [P, 4, NS])
        xgT_hi = sb("xgT_hi", [P, 2, CAP], F16)
        xgT_lo = sb("xgT_lo", [P, 2, CAP], F16)
        gelu = sb("gelu", [P, 2, CAP])
        hid = sb("hid", [P, 2, IC, CAP])
        eo = sb("eo", [P, 2, NS, D])

        attn_loaded = sem("attn_loaded")
        ffn_loaded = sem("ffn_loaded")
        x_loaded = [sem(f"x_loaded{i}") for i in range(4)]
        dve_waited = sem("dve_waited")
        pool_waited = sem("pool_waited")
        consts_step = sem("consts_step")
        consts_ready = sem("consts_ready")
        prep_pe = sem("prep_pe")
        prep_act = sem("prep_act")
        ln1_step = sem("ln1_step")
        ln1_var = sem("ln1_var")
        ln1_rstd = sem("ln1_rstd")
        ln1_shift = sem("ln1_shift")
        ln1_done = sem("ln1_done")
        ln1_done_act = sem("ln1_done_act")
        ln1_turned = sem("ln1_turned")
        moments_done = sem("moments_done")
        xT_ready = sem("xT_ready")
        fold_pe = sem("fold_pe")
        fold_dve = sem("fold_dve")
        fold_pow = sem("fold_pow")
        fold_mean = sem("fold_mean")
        z_done = sem("z_done")
        z_copied = sem("z_copied")
        scores_done = sem("scores_done")
        max_step = sem("max_step")
        exp_done = sem("exp_done")
        rsums_done = sem("rsums_done")
        probs_turned = sem("probs_turned")
        probsT_ready = sem("probsT_ready")
        xT_now_loaded = [sem(f"xT_now_loaded{i}") for i in range(2)]
        vals_done = sem("vals_done")
        vals_copied = sem("vals_copied")
        f_done = sem("f_done")
        f_ready = sem("f_ready")
        f_squared = sem("f_squared")
        x2_ready = sem("x2_ready")
        x2_stats = sem("x2_stats")
        norm_aggr = sem("norm_aggr")
        norm_var = sem("norm_var")
        f_var = sem("f_var")
        norm_pow = sem("norm_pow")
        xr_less_mean = sem("xr_less_mean")
        xr_ready = sem("xr_ready")
        xr_stored = [sem(f"xr_stored{i}") for i in range(2)]
        xr_turned = sem("xr_turned")
        xrT_ready = sem("xrT_ready")
        xrT_kept = [sem(f"xrT_kept{i}") for i in range(2)]
        logits_done = sem("logits_done")
        soft_dve = [sem(f"soft_dve{i}") for i in range(2)]
        soft_exp = [sem(f"soft_exp{i}") for i in range(2)]
        score_stored = sem("score_stored")
        chunks_loaded = sem("chunks_loaded")
        score_turned = sem("score_turned")
        by_expert_ready = sem("by_expert_ready")
        counted = sem("counted")
        counts_summed = sem("counts_summed")
        search_step = sem("search_step")
        upper_ready = sem("upper_ready")
        sh_gate_done = sem("sh_gate_done")
        sh_up_done = sem("sh_up_done")
        sh_gelu = sem("sh_gelu")
        sh_up = sem("sh_up")
        sh_hid = sem("sh_hid")
        sh_out_done = sem("sh_out_done")
        sh_out_copied = sem("sh_out_copied")
        sh_stored = [sem(f"sh_stored{i}") for i in range(2)]
        rank_dve = sem("rank_dve")
        rank_pe = sem("rank_pe")
        rank_act = sem("rank_act")
        gu_loaded = [sem(f"gu_loaded{i}") for i in range(2)]
        down_loaded = [sem(f"down_loaded{i}") for i in range(2)]
        gu_hi_ready = sem("gu_hi_ready")
        gu_lo_ready = sem("gu_lo_ready")
        started_ready = sem("started_ready")
        looked_up = sem("looked_up")
        idx_step = sem("idx_step")
        gathered = [sem(f"gathered{i}") for i in range(2)]
        xg_turned = sem("xg_turned")
        xgT_hi_ready = sem("xgT_hi_ready")
        xgT_lo_ready = sem("xgT_lo_ready")
        kept = sem("kept")
        gate_done = sem("gate_done")
        up_done = sem("up_done")
        gelu_done = sem("gelu_done")
        hid_done = sem("hid_done")
        eo_done = sem("eo_done")
        tail_done = sem("tail_done")
        tail_scaled = sem("tail_scaled")
        eo_scaled = sem("eo_scaled")
        scattered = [sem(f"scattered{i}") for i in range(2)]
        sum_loaded = [sem(f"sum_loaded{i}") for i in range(4)]
        fin_step = sem("fin_step")
        fin_var = sem("fin_var")
        fin_pow = sem("fin_pow")
        fin_shift = sem("fin_shift")
        fin_normed = sem("fin_normed")
        fin_ready_pool = sem("fin_ready_pool")
        fin_ready_dve = sem("fin_ready_dve")
        stored = sem("stored")

        PER_MAX, PER_IDX = 3, 4
        SOFT = ((0, 3 * NT // 4), (3 * NT // 4, NT))
        SOFT_STEP = B + 3
        A_STEPS, A_LO, A_HI = B + 7, 8, B - 2
        E_TURN, E_LO, E_HI = 4, 4, E - 4

        x_v = x.rearrange("(t q) d -> q t d", q=P)
        out_v = out.rearrange("(t q) d -> q t d", q=P)
        acc_v = acc.rearrange("(t q) d -> q t d", q=P)
        table_v = table.rearrange("(t q) r -> q t r", q=P)
        acc_sb = xT[:, :].rearrange("p (t d) -> p t d", d=D)

        def normed(g, i, width):
            return xn[:, ds(g, 1), i, 0:width].rearrange("p a d -> p (a d)")

        block = ctx.enter_context(nc.Block())

        @block.sync
        def _(sp):
            for g in range(NG):
                if g >= 4:
                    sp.wait_ge(x_loaded[g % 4], 16 * (g // 4))
                sp.dma_start(x_sb[:, 4 * g:4 * g + 4, :], x_v[:, 4 * g:4 * g + 4, :]).then_inc(x_loaded[g % 4], 16)
            for e in range(2):
                sp.dma_start(w_gu[:, e, :], w_experts[e, :, 0:GU]).then_inc(gu_loaded[e], 16)
            for e in range(2):
                sp.dma_start(w_down[:, e, :], w_experts[e, :, GU:]).then_inc(down_loaded[e], 16)

            def load_now(n, k):
                need(sp, vals_done, n - 1)
                sp.dma_start(xT_now[:, k, :], xT[:, ds(256 * n, 256)]).then_inc(xT_now_loaded[k], 16)

            def body(h, k):
                if s := stage(h, k, -1, B):
                    load_now(s[0], s[2])
                if s := stage(h, k, 4, B):
                    n, _, kk = s
                    sp.wait_ge(xr_ready, n + 1)
                    sp.dma_start(table_v[:, ds(2 * n, 2), 0:D], xr[:, kk, :, :]).then_inc(xr_stored[kk], 16)
                if s := stage(h, k, 5, B):
                    n, _, kk = s
                    sp.wait_ge(xrT_ready, n + 1)
                    sp.dma_start(xT[:, ds(256 * n, 256)], xrT[:, kk, :]).then_inc(xrT_kept[kk], 16)

            sp.wait_ge(xT_ready, NG)
            load_now(0, 0)
            pipeline(sp, body, A_STEPS, A_LO, A_HI)

            for p in range(2):
                sp.wait_ge(soft_dve[p], 5)
            sp.dma_start(table_v[:, :, D:ROW], score[:, :, :]).then_inc(score_stored, 16)
            sp.wait_ge(score_stored, 16)
            sp.dma_start(chunked[:, :, :],
                         table.rearrange("(p j) r -> p j r", j=32)[:, :, D:ROW]).then_inc(chunks_loaded, 16)
            with sp.Fori(0, NG // 2) as h:
                for k in range(2):
                    g = 2 * h + k
                    sp.wait_ge(sh_out_copied, g + 1)
                    sp.dma_start(acc_v[:, ds(4 * g, 4), :], sout[:, k, :, :]).then_inc(sh_stored[k], 16)
            def load_gate_up(e, k):
                sp.wait_ge(gu_hi_ready, e - 1)
                sp.wait_ge(gu_lo_ready, e - 1)
                sp.dma_start(w_gu[:, k, :], w_experts[ds(e, 1), :, 0:GU].rearrange("a p n -> p (a n)")
                             ).then_inc(gu_loaded[k], 16)

            def load_down(e, k):
                sp.wait_ge(eo_done, e - 1)
                sp.dma_start(w_down[:, k, :], w_experts[ds(e, 1), :, GU:].rearrange("a p n -> p (a n)")
                             ).then_inc(down_loaded[k], 16)

            load_gate_up(2, 0)
            with sp.Fori(1, E // 2 - 1) as h:
                for k in range(2):
                    load_gate_up(2 * h + k + 1, 1 - k)
                    load_down(2 * h + k, k)
            load_gate_up(E - 1, 1)
            load_down(E - 2, 0)
            load_down(E - 1, 1)
            for k in range(2):
                sp.wait_ge(scattered[k], 16 * NS * (E // 2))
            for g in range(NG):
                if g >= 4:
                    sp.wait_ge(sum_loaded[g % 4], 16 * (g // 4))
                sp.dma_start(acc_sb[:, 4 * g:4 * g + 4, :], acc_v[:, 4 * g:4 * g + 4, :]).then_inc(sum_loaded[g % 4], 16)
            for g in range(NG):
                sp.wait_ge(fin_ready_pool, g + 1)
                sp.wait_ge(fin_ready_dve, g + 1)
                sp.dma_start(out_v[:, 4 * g:4 * g + 4, :], x_sb[:, 4 * g:4 * g + 4, :]).then_inc(stored, 16)
            sp.wait_ge(stored, 16 * NG)

        @block.gpsimd
        def _(pool):
            done = [0]

            def step(ins):
                done[0] += 1
                ins.then_inc(consts_step, 1)
                pool.wait_ge(consts_step, done[0])

            def diagonal(tile, value, base, fill_where=ALU.not_equal):
                return nc.gpsimd.affine_select(out=tile, in_=tile, compare_op=fill_where, fill=value, base=base,
                                               pattern=[[-1, tile.shape[-1]]], channel_multiplier=1)

            step(nc.gpsimd.memset(neg_half[:], -0.5))
            step(nc.gpsimd.memset(ident[:], 0.0))
            step(diagonal(ident[:, :], 1.0, 0))
            step(nc.gpsimd.tensor_copy(ident16[:], ident[:]))
            step(nc.gpsimd.memset(causal[:], 0.0))
            for lo in (0, 256):
                step(nc.gpsimd.affine_select(out=causal[:, lo:lo + P], in_=causal[:, lo:lo + P], compare_op=ALU.is_ge,
                                             fill=MASKED, base=0, pattern=[[-1, P]], channel_multiplier=1))
            step(nc.gpsimd.memset(ones16[:], 1.0))
            nc.gpsimd.memset(ones[:], 1.0).then_inc(consts_ready, 1)

            def first(h, k):
                if s := stage(h, k, 0, NG):
                    g = s[0]
                    pool.wait_ge(ln1_var, g + 1)
                    need(pool, ln1_done_act, 2 * (g - 1))
                    nc.gpsimd.tensor_tensor(rstd[:, k, :], veps[:, k, :], neg_half[:, :],
                                            ALU.pow).then_inc(ln1_rstd, 1)

            pipeline(pool, first, NG, 2, NG)
            pool.wait_ge(fold_dve, 6)
            nc.gpsimd.tensor_tensor(bn[:, 4, :], bn[:, 3, :], neg_half[:, 0:3], ALU.pow).then_inc(fold_pow, 1)

            step(nc.gpsimd.affine_select(out=before[:, :], in_=ones16[:, :], compare_op=ALU.is_gt, fill=0.0, base=0,
                                         pattern=[[1, P]], channel_multiplier=-1))
            step(nc.gpsimd.memset(shift[:], 0.0))
            step(diagonal(shift[:, :], 1.0, 1))
            step(nc.gpsimd.memset(differ[:], 0.0))
            step(diagonal(differ[:, :], 1.0, 0))
            step(diagonal(differ[:, :], -1.0, 1))
            step(nc.gpsimd.memset(same_expert[:], 0.0))
            for off in range(-(P // E) + 1, P // E):
                step(diagonal(same_expert[:, :], 1.0, E * off))
            step(nc.gpsimd.iota(digits[:], pattern=[[0, DIGITS + 1], [1, 3]], base=1, channel_multiplier=0))
            step(nc.gpsimd.iota(digit_shift[:], pattern=[[-2, DIGITS + 1], [0, 3]], base=2 * DIGITS - 2,
                                channel_multiplier=0))
            step(nc.gpsimd.iota(place_shift[:, 0, :, :], pattern=[[-2, DIGITS], [0, 3]], base=2 * DIGITS - 2 - FOUR_BIT,
                                channel_multiplier=0))
            step(nc.gpsimd.iota(place_shift[:, 1, :, :], pattern=[[2, DIGITS], [0, 3]], base=FOUR_BIT - 2 * DIGITS + 2,
                                channel_multiplier=0))
            step(nc.gpsimd.memset(four[:], 4.0))
            step(nc.gpsimd.iota(slot_row[:], pattern=[[1, CAP]], base=0, channel_multiplier=0,
                                allow_small_or_imprecise_dtypes=True))
            step(nc.gpsimd.iota(slot_col[:], pattern=[[P, NS], [0, 32]], base=0, channel_multiplier=1,
                                allow_small_or_imprecise_dtypes=True))
            step(nc.gpsimd.memset(scan_keep[:], 1.0))
            step(nc.gpsimd.memset(scan_keep[:, :, 0:1], 0.0))
            nc.gpsimd.memset(rank_steps[:, :, 32:33], 1.0).then_inc(consts_ready, 1)

            def body(h, k):
                if s := stage(h, k, 4, B):
                    n, hh, kk = s
                    pool.wait_ge(norm_var, n + 2)
                    need(pool, xr_turned, n - 1)
                    need(pool, xr_stored[kk], 16 * hh)
                    nc.gpsimd.tensor_tensor(xr[:, kk, :, :], x_sb[:, ds(2 * n, 2), :],
                                            mv2[:, 1 - kk, :, 0:1].to_broadcast([P, 2, D]),
                                            ALU.subtract).then_inc(xr_less_mean, 1)
                    pool.wait_ge(xr_less_mean, n + 1)
                    pool.wait_ge(norm_pow, n + 2)
                    nc.gpsimd.tensor_tensor(xr[:, kk, :, :], xr[:, kk, :, :],
                                            rstd2[:, 1 - kk, 2:4].unsqueeze(2).to_broadcast([P, 2, D]),
                                            ALU.mult).then_inc(xr_ready, 1)
                if s := stage(h, k, 2, B + 2):
                    n, _, kk = s
                    if not isinstance(n, int) or n < B:
                        pool.wait_ge(f_squared, 2 * n + 2)
                    need(pool, norm_pow, n - 1)
                    pool.sem_inc(pool_waited, 1)
                    nc.gpsimd.tensor_scalar(veps2[:, kk, 0:2], square_sum[:, kk, :], 1.0 / D, EPS, ALU.mult,
                                            ALU.add).then_inc(f_var, 1)
                    pool.wait_ge(f_var, n + 1)
                    pool.wait_ge(norm_var, n + 1)
                    need(pool, xr_ready, n - 2)
                    nc.gpsimd.tensor_tensor(rstd2[:, kk, :], veps2[:, kk, :], neg_half[:, :],
                                            ALU.pow).then_inc(norm_pow, 1)

            pipeline(pool, body, A_STEPS, A_LO, A_HI)

            with pool.Fori(0, NG // 2) as h:
                for k in range(2):
                    g = 2 * h + k
                    for c in range(SC):
                        pool.wait_ge(sh_gelu, SC * g + c + 1)
                        pool.wait_ge(sh_up, SC * g + c + 1)
                        nc.gpsimd.tensor_tensor(shid[:, k, c, :], sgelu[:, c, :], sup[:, c, :],
                                                ALU.mult).then_inc(sh_hid, 1)

            def gather(s):
                n, _, k4 = s
                k = k4 % 2
                pool.wait_ge(score_stored, 16)
                pool.wait_ge(idx_step, PER_IDX * (n + 1))
                need(pool, xg_turned, n - 1)
                need(pool, kept, n - 1)
                pool.sem_inc(pool_waited, 1)
                for t in range(NS):
                    nc.gpsimd.indirect_dma_start(
                        out=xg[:, k, t, :], out_offset=None, in_=table[:, :],
                        in_offset=bass.IndirectOffsetOnAxis(ap=idx_in[:, k4, t:t + 1], axis=0)).then_inc(gathered[k], 16)

            def scatter(s):
                n, h, k4 = s
                k, pair = k4 % 2, 2 * h + k4 // 2
                for g in range(2):
                    pool.wait_ge(sh_stored[g], 16 * (NG // 2))
                tail = isinstance(n, int) and n == E - 1
                if not tail:
                    pool.wait_ge(eo_scaled, 2 * (n + 1))
                if k == 0:
                    need(pool, scattered[1], 16 * NS * pair)
                else:
                    pool.wait_ge(scattered[0], 16 * NS * (pair + 1))
                pool.sem_inc(pool_waited, 1)
                for t in range(NS):
                    if tail:
                        pool.wait_ge(tail_scaled, t + 2)
                    nc.gpsimd.indirect_dma_start(
                        out=acc[:, :], out_offset=bass.IndirectOffsetOnAxis(ap=idx_out[:, k4, t:t + 1], axis=0),
                        in_=eo[:, k, t, :], in_offset=None, compute_op=ALU.add).then_inc(scattered[k], 16)

            def experts(h, k):
                if s := stage(h, k, -2, E, E_TURN):
                    gather(s)
                if s := stage(h, k, 1, E, E_TURN):
                    scatter(s)

            for b in range(2):
                pool.wait_ge(xr_stored[b], 16 * (B // 2))
            gather((0, 0, 0))
            gather((1, 0, 1))
            pipeline(pool, experts, E + 1, E_LO, E_HI, E_TURN)

            def last(h, k):
                if s := stage(h, k, 0, NG):
                    g, _, kk = s
                    pool.wait_ge(fin_var, g + 1)
                    need(pool, fin_normed, 4 * (g - 1))
                    nc.gpsimd.tensor_tensor(rstd[:, kk, :], veps[:, kk, :], neg_half[:, :],
                                            ALU.pow).then_inc(fin_pow, 1)
                if s := stage(h, k, 1, NG):
                    g = s[0]
                    pool.wait_ge(fin_normed, 4 * g + 2)
                    t = ds(4 * g, 2)
                    nc.gpsimd.tensor_tensor(x_sb[:, t, :], x_sb[:, t, :], acc_sb[:, t, :],
                                            ALU.add).then_inc(fin_ready_pool, 1)

            pipeline(pool, last, NG + 1, 2, NG)

        @block.tensor
        def _(pe):
            pe.wait_ge(consts_ready, 1)

            def prepare(part):
                if part == 0:
                    pe.wait_ge(attn_loaded, 16 * 2)
                    nc.tensor.matmul(bank[3][:, 0:384], ident[:, :], wa[:, :], start=True, stop=False)
                    nc.tensor.matmul(bank[3][:, 0:384], aat[:, :], ab[:, :], start=False, stop=True).then_inc(prep_pe, 1)
                    nc.tensor.matmul(bank[4][:, 0:D], ident[:, :], wp[:, :], start=True, stop=False)
                    nc.tensor.matmul(bank[4][:, 0:D], pat[:, :], pb[:, :], start=False, stop=True).then_inc(prep_pe, 1)
                elif part == 1:
                    pe.wait_ge(prep_act, 2)
                    for j in range(3):
                        last = nc.tensor.transpose(bank[5][:, j * P:(j + 1) * P], wm_raw[:, j * D:(j + 1) * D],
                                                   ident[:, :])
                    last.then_inc(prep_pe, 1)
                    nc.tensor.transpose(bank[6][:, 0:P], wmp[:, :], ident[:, :]).then_inc(prep_pe, 1)
                else:
                    pe.wait_ge(prep_act, 4)
                    for j in range(3):
                        last = nc.tensor.transpose(bank[3][:, j * P:(j + 1) * P], wmT[:, j * D:(j + 1) * D],
                                                   ident[:, :])
                    last.then_inc(prep_pe, 1)
                    nc.tensor.matmul(bank[4][:, 0:D], wp[:, :], wmpT[:, :], start=True, stop=True).then_inc(prep_pe, 1)

            prepare(0)
            for g in range(NG):
                pe.wait_ge(ln1_done, 2 * g + 2)
                pe.wait_ge(ln1_done_act, 2 * g + 2)
                if g >= 2:
                    pe.wait_ge(xT_ready, g - 1)
                for part in (("turn", "moments") if g < NG - 1 else ("moments", "turn")):
                    for j in range(4):
                        if part == "turn":
                            last = nc.tensor.transpose(bank[g % 2][:, j * P:(j + 1) * P], xn[:, g, j, 0:D],
                                                       ident[:, :])
                        else:
                            last = nc.tensor.matmul(bank[2][:, 0:D + 1], xn[:, g, j, 0:D], xn[:, g, j, :],
                                                    start=g == 0 and j == 0, stop=g == NG - 1 and j == 3)
                    if part == "turn":
                        last.then_inc(ln1_turned, 1)
                    elif g == NG - 1:
                        last.then_inc(moments_done, 1)
                if g < 2:
                    prepare(g + 1)

            pe.wait_ge(fold_dve, 1)
            nc.tensor.matmul(bank[3][:, 0:384], gram[:, 0:D], wmT[:, :], start=True, stop=True).then_inc(fold_pe, 1)
            for j in range(3):
                last = nc.tensor.matmul(bank[4][:, j:j + 1], wmT[:, j * D:(j + 1) * D], gram[:, D:D + 1],
                                        start=True, stop=True)
            last.then_inc(fold_pe, 1)
            pe.wait_ge(fold_dve, 2)
            for j in range(3):
                last = nc.tensor.matmul(bank[5][:, j:j + 1], wgram[:, j * D:(j + 1) * D], ones[:, 0:1],
                                        start=True, stop=True)
            last.then_inc(fold_pe, 1)
            pe.wait_ge(fold_dve, 9)
            nc.tensor.matmul(bank[3][:, 0:D], wns[:, 0, :], wns[:, 1, :], start=True, stop=True).then_inc(fold_pe, 1)
            pe.wait_ge(fold_dve, 11)
            pe.wait_ge(fold_mean, 2)
            nc.tensor.matmul(bank[5][:, 0:D], wns[:, 2, :], p2T[:, :], start=True, stop=True).then_inc(fold_pe, 1)
            pe.wait_ge(fold_dve, 12)
            nc.tensor.matmul(bank[4][:, 0:1], wns[:, 1, :], bn[:, 7, 0:1], start=True, stop=True).then_inc(fold_pe, 1)

            pe.wait_ge(xT_ready, NG)
            pe.wait_ge(ffn_loaded, 16)

            def body(h, k):
                s0, s1, s2 = stage(h, k, 0, B), stage(h, k, 1, B), stage(h, k, 2, B)
                if s0:
                    n, _, kk = s0
                    sp_bank = bank[1 + kk]
                    need(pe, exp_done, 2 * (n - 1))
                    nc.tensor.matmul(sp_bank[:, 0:384], ident16[:, :], causal[:, :], start=True, stop=False)
                    pe.wait_ge(z_copied, n + 1)
                    nc.tensor.matmul(sp_bank[:, 0:P], zT[:, kk, 0:P], xT[:, ds(256 * n, P)], start=False, stop=False)
                    nc.tensor.matmul(sp_bank[:, P:384], zT[:, kk, P:256], xT[:, ds(256 * n, 256)],
                                     start=False, stop=True).then_inc(scores_done, 1)
                if s2:
                    n, _, kk = s2
                    pe.wait_ge(probsT_ready, n + 1)
                    pe.wait_ge(vals_copied, n + 1)
                    need(pe, f_ready, 2 * n)
                    nc.tensor.matmul(bank[5][:, 0:P], probsT[:, kk, 0:P], vals[:, kk, 0:P], start=True, stop=True)
                    nc.tensor.matmul(bank[5][:, P:256], probsT[:, kk, P:256], vals[:, kk, 0:P],
                                     start=True, stop=False)
                    nc.tensor.matmul(bank[5][:, P:256], probsT[:, kk, 256:384], vals[:, kk, P:256],
                                     start=False, stop=True).then_inc(f_done, 1)
                if s1:
                    n, _, kk = s1
                    pe.wait_ge(exp_done, 2 * n + 2)
                    need(pe, probsT_ready, n)
                    for j in range(3):
                        last = nc.tensor.transpose(bank[3][:, j * P:(j + 1) * P], probs[:, kk, j * P:(j + 1) * P],
                                                   ident[:, :])
                    last.then_inc(probs_turned, 1)
                if s := stage(h, k, -1, B):
                    turn_queries(s[0])
                if s := stage(h, k, 5, B):
                    n, _, kk = s
                    pe.wait_ge(xr_ready, n + 1)
                    need(pe, xrT_ready, n)
                    for j in range(2):
                        last = nc.tensor.transpose(bank[6][:, j * P:(j + 1) * P], xr[:, kk, j, :], ident[:, :])
                    last.then_inc(xr_turned, 1)
                if s0:
                    n, hh, kk = s0
                    if isinstance(n, int) and n == 0:
                        pe.wait_ge(fold_dve, 17)
                    pe.wait_ge(xT_now_loaded[kk], 16 * (hh + 1))
                    need(pe, vals_copied, n)
                    for j in range(2):
                        last = nc.tensor.matmul(bank[4][:, j * P:(j + 1) * P], xT_now[:, kk, j * P:(j + 1) * P],
                                                outw[:, 0, :], start=True, stop=True)
                    last.then_inc(vals_done, 1)
                if s := stage(h, k, 6, B):
                    n, _, kk = s
                    pe.wait_ge(xrT_ready, n + 1)
                    if isinstance(n, int) and 2 * n >= SOFT[1][0]:
                        pe.wait_ge(z_copied, B)
                        logits, m = bank[0], n - SOFT[1][0] // 2
                    else:
                        logits, m = bank[7], n
                    for j in range(2):
                        last = nc.tensor.matmul(logits[:, ds(2 * E * m + E * j, E)], xrT[:, kk, j * P:(j + 1) * P],
                                                gate[:, :], start=True, stop=True)
                    last.then_inc(logits_done, 1)

            def turn_queries(n):
                need(pe, z_copied, n)
                nc.tensor.matmul(bank[0][:, 0:256], mix[:, :], xT[:, ds(256 * n, 256)],
                                 start=True, stop=True).then_inc(z_done, 1)

            pe.wait_ge(fold_dve, 14)
            turn_queries(0)
            nc.tensor.matmul(bank[6][:, 0:D], bv_wide[:, :], p2T[:, :], start=True, stop=True).then_inc(fold_pe, 1)
            pipeline(pe, body, A_STEPS, A_LO, A_HI)

            for p in range(2):
                pe.wait_ge(soft_dve[p], 5)
            for a in range(4):
                last = nc.tensor.transpose(bank[0][:, a * P:(a + 1) * P],
                                           score[:, 8 * a:8 * a + 8, :].rearrange("p t e -> p (t e)"), ident[:, :])
            last.then_inc(score_turned, 1)
            for b in range(2):
                pe.wait_ge(xrT_kept[b], 16 * (B // 2))
            pe.wait_ge(consts_ready, 2)

            def shared(h, k):
                s0, s1 = stage(h, k, 0, NG), stage(h, k, 1, NG)

                def out_half(a):
                    if s1:
                        g, _, kk = s1
                        if a == 0:
                            pe.wait_ge(sh_hid, SC * (g + 1))
                            need(pe, sh_out_copied, g)
                        for j in range(2 * a, 2 * a + 2):
                            for c in range(SC):
                                last = nc.tensor.matmul(bank[5][:, j * D:(j + 1) * D],
                                                        shid[:, kk, c, j * P:(j + 1) * P], sd[:, c, :],
                                                        start=c == 0, stop=c == SC - 1)
                        if a == 1:
                            last.then_inc(sh_out_done, 1)

                def sum_counts(c):
                    if s0 and not (isinstance(s0[0], int) and SC * s0[0] + c >= DIGITS):
                        pe.wait_ge(counted, SC * s0[0] + c + 1)
                        nc.tensor.matmul(bank[6][:, 0:7], same_expert[:, :], count[:, :],
                                         start=True, stop=True).then_inc(counts_summed, 1)

                for c in range(SC):
                    if s0 and isinstance(s0[0], int) and SC * s0[0] + c == DIGITS:
                        pe.wait_ge(rank_dve, 1)
                        nc.tensor.transpose(bank[0][:, 0:E], least_wide[0:E, :], ident[0:E, 0:E]).then_inc(rank_pe, 1)
                    if s0:
                        g = s0[0]
                        cols = ds(512 * g, 512)
                        need(pe, sh_gelu, SC * (g - 1) + c + 1)
                        nc.tensor.matmul(bank[1 + c][:, :], sg[:, c * P:(c + 1) * P], xT[:, cols],
                                         start=True, stop=True).then_inc(sh_gate_done, 1)
                        need(pe, sh_up, SC * (g - 1) + c + 1)
                        nc.tensor.matmul(bank[3 + c][:, :], su[:, c * P:(c + 1) * P], xT[:, cols],
                                         start=True, stop=True).then_inc(sh_up_done, 1)
                    sum_counts(c)
                    out_half(c)

            pipeline(pe, shared, NG, 4, NG - 2)

            pe.wait_ge(rank_dve, 6)
            for i, a in enumerate((above_sum, equal_sum)):
                nc.tensor.matmul(bank[7][:, i * E:(i + 1) * E], before[:, :], a[:, :, 31], start=True, stop=True)
            nc.tensor.matmul(bank[7][:, 2 * E:3 * E], ones16[:, :], above_sum[:, :, 31],
                             start=True, stop=True).then_inc(rank_pe, 1)
            pe.wait_ge(rank_dve, 11)
            base_wide = chunk_base[:, :].unsqueeze(2).to_broadcast([P, E, 32])
            for i, a in enumerate((above_sum[:, :, :], equal_taken[:, :, :], base_wide)):
                last = nc.tensor.matmul(bank[0][:, :].rearrange("p (e j) -> p e j", j=32), differ[:, :], a,
                                        start=i == 0, stop=i == 2)
            last.then_inc(rank_pe, 1)
            for i, a in enumerate((above_sum[:, :, 31], equal_taken[:, :, 31], chunk_base[:, :])):
                last = nc.tensor.matmul(bank[6][:, 0:E], shift[:, :], a, start=i == 0, stop=i == 2)
            last.then_inc(rank_pe, 1)
            pe.wait_ge(rank_dve, 12)
            pe.wait_ge(rank_act, 1)

            def look_up(s):
                n, _, k = s
                pe.wait_ge(started_ready, n + 1)
                need(pe, idx_step, PER_IDX * n)
                for t in range(NS):
                    last = nc.tensor.matmul(bank[0][:, t * 33:t * 33 + 33], started[:, k % 2, t * P:(t + 1) * P],
                                            rank_steps[:, ds(n, 1), :].rearrange("p a j -> p (a j)"),
                                            start=True, stop=True)
                last.then_inc(looked_up, 1)

            def turn_tokens(s):
                n, h, k = s
                pe.wait_ge(gathered[k % 2], 16 * NS * (2 * h + k // 2 + 1))
                need(pe, xgT_lo_ready, n)
                for t in range(NS):
                    last = nc.tensor.transpose(bank[1][:, t * P:(t + 1) * P], xg[:, k % 2, t, 0:D], ident[:, :])
                last.then_inc(xg_turned, 1)

            def product(dst, k, c):
                cols = slice(c * P, (c + 1) * P)
                nc.tensor.matmul(dst, w_gu_hi[:, k, cols], xgT_hi[:, k, :], start=True, stop=False)
                nc.tensor.matmul(dst, w_gu_hi[:, k, cols], xgT_lo[:, k, :], start=False, stop=False)
                return nc.tensor.matmul(dst, w_gu_lo[:, k, cols], xgT_hi[:, k, :], start=False, stop=True)

            def gate_up(s, c):
                n, _, k = s
                if c == 0:
                    pe.wait_ge(gu_lo_ready, n + 1)
                    pe.wait_ge(gu_hi_ready, n + 1)
                    pe.wait_ge(xgT_hi_ready, n + 1)
                    pe.wait_ge(xgT_lo_ready, n + 1)
                need(pe, gelu_done, IC * n + c - 1)
                product(bank[2 + c % 2][:, :], k % 2, c).then_inc(gate_done, 1)
                need(pe, hid_done, IC * n + c - 1)
                product(bank[4 + c % 2][:, :], k % 2, IC + c).then_inc(up_done, 1)

            def down(s):
                n, h, k4 = s
                k = k4 % 2
                pe.wait_ge(down_loaded[k], 16 * (2 * h + k4 // 2 + 1))
                pe.wait_ge(hid_done, IC * (n + 1))
                need(pe, eo_scaled, 2 * (n - 1))
                for t in range(NS):
                    tail = isinstance(n, int) and n == E - 1
                    made = bank[2 + t][:, 0:D] if tail else bank[6 + k][:, t * D:(t + 1) * D]
                    for c in range(IC):
                        last = nc.tensor.matmul(made, hid[:, k, c, t * P:(t + 1) * P],
                                                w_down[:, k, c * P:(c + 1) * P], start=c == 0, stop=c == IC - 1)
                    if tail:
                        last.then_inc(tail_done, 1)
                if not tail:
                    last.then_inc(eo_done, 1)

            def experts(h, k):
                this = stage(h, k, 0, E, E_TURN)
                if this:
                    gate_up(this, 0)
                if s := stage(h, k, 1, E, E_TURN):
                    down(s)
                if this:
                    gate_up(this, 1)
                if s := stage(h, k, -1, E, E_TURN):
                    turn_tokens(s)
                if this:
                    gate_up(this, 2)
                if s := stage(h, k, -3, E, E_TURN):
                    look_up(s)
                if this:
                    gate_up(this, 3)

            for n in range(3):
                look_up((n, 0, n))
            shared(NG // 2, 0)
            turn_tokens((0, 0, 0))
            pipeline(pe, experts, E + 1, E_LO, E_HI, E_TURN)

        @block.scalar
        def _(act):
            act.dma_start(low_rank[:, :], low_rank_in).then_inc(attn_loaded, 16)
            act.dma_start(attn_w[:, :], attn_w_in).then_inc(attn_loaded, 16)
            act.dma_start(ffn_w[:, :], ffn_w_in).then_inc(ffn_loaded, 16)

            def prepare(part):
                if part == 0:
                    act.wait_ge(prep_pe, 2)
                    nc.scalar.activation(wm_raw[:, :], bank[3][:, 0:384], ACT.Copy).then_inc(prep_act, 1)
                    nc.scalar.activation(wmp[:, :], bank[4][:, 0:D], ACT.Copy).then_inc(prep_act, 1)
                elif part == 1:
                    act.wait_ge(prep_pe, 4)
                    nc.scalar.activation(wmT[:, :].rearrange("p (r k) -> p k r", k=3),
                                         bank[5][:, 0:384].rearrange("p (k r) -> p k r", k=3),
                                         ACT.Copy).then_inc(prep_act, 1)
                    nc.scalar.activation(wmpT[:, :], bank[6][:, 0:P], ACT.Copy).then_inc(prep_act, 1)
                else:
                    act.wait_ge(prep_pe, 6)
                    nc.scalar.activation(wn[:, :, :], bank[3][:, 0:384].rearrange("p (k r) -> p k r", k=3),
                                         ACT.Copy).then_inc(prep_act, 1)
                    nc.scalar.activation(p2T_raw[:, :], bank[4][:, 0:D], ACT.Copy).then_inc(prep_act, 1)

            def first_norm(h, k):
                if s := stage(h, k, 0, NG):
                    g, _, kk = s
                    act.wait_ge(ln1_shift, g + 1)
                    for i in range(2, 4):
                        nc.scalar.activation(normed(g, i, D), x_sb[:, ds(4 * g + i, 1), :].rearrange("p a d -> p (a d)"),
                                             ACT.Identity, bias=shiftm[:, kk, i:i + 1],
                                             scale=rstd[:, kk, i:i + 1]).then_inc(ln1_done_act, 1)
                    if isinstance(g, int) and g == 0:
                        prepare(0)
                if s := stage(h, k, 1, NG):
                    g, _, kk = s
                    act.wait_ge(ln1_turned, g + 1)
                    nc.scalar.activation(xT[:, ds(512 * g, 512)], bank[kk][:, :], ACT.Copy).then_inc(xT_ready, 1)
                    if isinstance(g, int) and g < 2:
                        prepare(g + 1)

            pipeline(act, first_norm, NG + 1, 4, NG)

            def body(h, k):
                s0 = stage(h, k, 0, B)
                if s := stage(h, k, 1, B):
                    n, _, kk = s
                    act.wait_ge(probs_turned, n + 1)
                    need(act, f_done, n - 1)
                    nc.scalar.activation(probsT[:, kk, :], bank[3][:, 0:384], ACT.Copy).then_inc(probsT_ready, 1)
                if s := stage(h, k, -1, B):
                    copy_queries(s[0], s[2])
                if s0:
                    n, _, kk = s0
                    act.wait_ge(max_step, PER_MAX * (n + 1))
                    need(act, probs_turned, n - 1)
                    need(act, rsums_done, n - 1)
                    for j, (lo, hi) in enumerate(((0, P), (P, 384))):
                        nc.scalar.activation(probs[:, kk, lo:hi], bank[1 + kk][:, lo:hi], ACT.Exp,
                                             bias=nbias[:, kk, j:j + 1], scale=SCALE,
                                             accum_out=psums[:, kk, j:j + 1]).then_inc(exp_done, 1)
                    act.wait_ge(vals_done, n + 1)
                    need(act, f_done, n - 1)
                    nc.scalar.activation(vals[:, kk, :], bank[4][:, 0:256], ACT.Copy).then_inc(vals_copied, 1)
                if s := stage(h, k, 5, B):
                    n, hh, kk = s
                    act.wait_ge(xr_turned, n + 1)
                    need(act, logits_done, n - 1)
                    need(act, xrT_kept[kk], 16 * hh)
                    nc.scalar.activation(xrT[:, kk, :], bank[6][:, 0:256], ACT.Copy).then_inc(xrT_ready, 1)
                if s := stage(h, k, 2, B):
                    n, _, kk = s
                    act.wait_ge(f_ready, 2 * (n + 1))
                    need(act, f_var, n - 1)
                    for j in range(2):
                        need(act, f_squared, 2 * n + j)
                        nc.scalar.activation(squares[:, :], f[:, kk, j, :], ACT.Square,
                                             accum_out=square_sum[:, kk, j:j + 1]).then_inc(f_squared, 1)
                if isinstance(h, int) and 2 * h + k == SOFT_STEP:
                    soft_exponents(0)

            def soft_exponents(p):
                act.wait_ge(soft_dve[p], 2)
                lo, hi = SOFT[p]
                nc.scalar.activation(logit[:, lo:hi, :], logit[:, lo:hi, :], ACT.Exp).then_inc(soft_exp[p], 1)

            def copy_queries(n, k):
                act.wait_ge(z_done, n + 1)
                need(act, scores_done, n - 1)
                nc.scalar.activation(zT[:, k, :], bank[0][:, 0:256], ACT.Identity,
                                     bias=mix_bias[:, 0:1]).then_inc(z_copied, 1)

            act.wait_ge(fold_dve, 15)
            copy_queries(0, 0)
            pipeline(act, body, A_STEPS, A_LO, A_HI)

            soft_exponents(1)
            act.wait_ge(score_turned, 1)
            nc.scalar.activation(by_expert[:, :], bank[0][:, :], ACT.Copy).then_inc(by_expert_ready, 1)

            def shared(h, k):
                if s := stage(h, k, 0, NG):
                    g = s[0]
                    for c in range(SC):
                        act.wait_ge(sh_gate_done, SC * g + c + 1)
                        need(act, sh_hid, SC * (g - 1) + c + 1)
                        nc.scalar.activation(sgelu[:, c, :], bank[1 + c][:, :], ACT.Gelu).then_inc(sh_gelu, 1)
                        act.wait_ge(sh_up_done, SC * g + c + 1)
                        nc.scalar.activation(sup[:, c, :], bank[3 + c][:, :], ACT.Copy).then_inc(sh_up, 1)
                if s := stage(h, k, 1, NG):
                    g, hh, kk = s
                    act.wait_ge(sh_out_done, g + 1)
                    need(act, sh_stored[kk], 16 * hh)
                    nc.scalar.activation(sout[:, kk, :, :], bank[5][:, :].rearrange("p (j d) -> p j d", d=D),
                                         ACT.Copy).then_inc(sh_out_copied, 1)

            pipeline(act, shared, NG, 4, NG)

            def weights_hi(s):
                n, h, k4 = s
                k = k4 % 2
                act.wait_ge(gu_loaded[k], 16 * (2 * h + k4 // 2 + 1))
                need(act, up_done, IC * (n - 1))
                nc.scalar.activation(w_gu_hi[:, k, :], w_gu[:, k, :], ACT.Copy, scale=W_UP).then_inc(gu_hi_ready, 1)

            def tokens_hi(s):
                n, _, k = s
                act.wait_ge(xg_turned, n + 1)
                need(act, up_done, IC * (n - 1))
                nc.scalar.activation(xgT_hi[:, k % 2, :], bank[1][:, :], ACT.Copy).then_inc(xgT_hi_ready, 1)

            def experts(h, k):
                this, following = stage(h, k, 0, E, E_TURN), stage(h, k, -1, E, E_TURN)

                def gelus(c):
                    n = this[0]
                    act.wait_ge(gate_done, IC * n + c + 1)
                    need(act, hid_done, IC * n + c - 1)
                    nc.scalar.activation(gelu[:, c % 2, :], bank[2 + c % 2][:, :], ACT.Gelu,
                                         scale=1.0 / W_UP).then_inc(gelu_done, 1)

                gelus(0)
                if following:
                    weights_hi(following)
                gelus(1)
                if following:
                    tokens_hi(following)
                gelus(2)
                gelus(3)

            weights_hi((0, 0, 0))
            act.wait_ge(rank_pe, 3)
            nc.scalar.activation(rank_steps[:, :, 0:32], bank[0][:, :].rearrange("p (e j) -> p e j", j=32),
                                 ACT.Copy).then_inc(rank_act, 1)
            shared(NG // 2, 0)
            tokens_hi((0, 0, 0))
            pipeline(act, experts, E, E_LO, E_HI, E_TURN)

            def last_norm(h, k):
                g, _, kk = stage(h, k, 0, NG)
                act.wait_ge(fin_shift, g + 1)
                for i in range(4):
                    v = acc_sb[:, ds(4 * g + i, 1), :].rearrange("p a d -> p (a d)")
                    nc.scalar.activation(v, v, ACT.Identity, bias=shiftm[:, kk, i:i + 1],
                                         scale=rstd[:, kk, i:i + 1]).then_inc(fin_normed, 1)

            pipeline(act, last_norm, NG, 2, NG)

        @block.vector
        def _(dve):
            nc.vector.memset(xn[:, :, :, D:D + 1], 1.0).then_inc(ln1_step, 1)
            nc.vector.memset(stat2[:, :, :, :], 1.0).then_inc(ln1_step, 1)

            LN1 = 8

            def stats(h, j, k):
                g = 4 * h + j
                dve.wait_ge(x_loaded[j], 16 * (h + 1))
                for i in range(4):
                    nc.vector.bn_stats(stat[:, k, i, :],
                                       x_sb[:, ds(4 * g + i, 1), :].rearrange("p a d -> p (a d)")).then_inc(ln1_step, 1)
                dve.wait_ge(ln1_step, 2 + LN1 * g + 4)
                dve.sem_inc(dve_waited, 1)
                for i in range(4):
                    nc.vector.bn_aggr(mv[:, k, i, :], stat[:, k, i, :]).then_inc(ln1_step, 1)
                before_this = not isinstance(g, int) or g >= 1
                if before_this:
                    shift_and_norm(g - 1, 1 - k, 0)
                dve.wait_ge(ln1_step, 2 + LN1 * (g + 1))
                nc.vector.tensor_scalar(veps[:, k, :], mv[:, k, :, 1], EPS, None, ALU.add).then_inc(ln1_var, 1)
                if before_this:
                    shift_and_norm(g - 1, 1 - k, 1)

            def shift_and_norm(g, k, i):
                if i == 0:
                    dve.wait_ge(ln1_rstd, g + 1)
                    need(dve, ln1_done_act, 2 * (g - 1))
                    nc.vector.scalar_tensor_tensor(out=shiftm[:, k, :], in0=mv[:, k, :, 0], scalar=-1.0,
                                                   in1=rstd[:, k, :], op0=ALU.mult, op1=ALU.mult).then_inc(ln1_shift, 1)
                nc.vector.tensor_scalar(normed(g, i, D), x_sb[:, ds(4 * g + i, 1), :].rearrange("p a d -> p (a d)"),
                                        mv[:, k, i, 0:1], rstd[:, k, i:i + 1], ALU.subtract,
                                        ALU.mult).then_inc(ln1_done, 1)

            for g in range(4):
                stats(0, g, g % 2)
            with dve.Fori(1, NG // 4) as h:
                for j in range(4):
                    stats(h, j, j % 2)
            dve.wait_ge(prep_act, 6)
            nc.vector.tensor_reduce(p2T_mean[:, :], p2T_raw[:, :], AX, ALU.add).then_inc(fold_mean, 1)
            dve.wait_ge(fold_mean, 1)
            nc.vector.scalar_tensor_tensor(out=p2T[:, :], in0=p2T_mean[:, :].to_broadcast([P, D]), scalar=-1.0 / D,
                                           in1=p2T_raw[:, :], op0=ALU.mult, op1=ALU.add).then_inc(fold_mean, 1)
            for i in range(2):
                shift_and_norm(NG - 1, (NG - 1) % 2, i)

            dve.wait_ge(moments_done, 1)
            nc.vector.tensor_scalar(gram[:, :], bank[2][:, 0:D + 1], 1.0 / TOK, None, ALU.mult).then_inc(fold_dve, 1)
            dve.wait_ge(fold_pe, 1)
            dve.wait_ge(prep_act, 6)
            nc.vector.tensor_tensor(wgram[:, :], bank[3][:, 0:384], wmT[:, :], ALU.mult).then_inc(fold_dve, 1)
            dve.wait_ge(fold_pe, 2)
            nc.vector.tensor_copy(bn[:, 0, :], bank[4][:, 0:3]).then_inc(fold_dve, 1)
            dve.wait_ge(fold_dve, 3)
            nc.vector.tensor_tensor(bn[:, 1, :], bn[:, 0, :], bn[:, 0, :], ALU.mult).then_inc(fold_dve, 1)
            dve.wait_ge(fold_pe, 3)
            dve.wait_ge(fold_dve, 4)
            nc.vector.tensor_tensor(bn[:, 2, :], bank[5][:, 0:3], bn[:, 1, :], ALU.subtract).then_inc(fold_dve, 1)
            dve.wait_ge(fold_dve, 5)
            nc.vector.tensor_scalar(bn[:, 3, :], bn[:, 2, :], 0.0, EPS, ALU.max, ALU.add).then_inc(fold_dve, 1)
            dve.wait_ge(fold_pow, 1)
            nc.vector.tensor_tensor(bn[:, 5, :], bn[:, 4, :], gamma[:, :], ALU.mult).then_inc(fold_dve, 1)
            dve.wait_ge(fold_dve, 7)
            for j in range(2):
                nc.vector.tensor_scalar(wns[:, j, :], wn[:, j, :], bn[:, 5, j:j + 1], None, ALU.mult).then_inc(fold_dve, 1)
            nc.vector.tensor_tensor(bn[:, 6, :], bn[:, 0, :], bn[:, 5, :], ALU.mult).then_inc(fold_dve, 1)
            nc.vector.tensor_scalar(wns[:, 2, :], wn[:, 2, :], bn[:, 5, 2:3], None, ALU.mult).then_inc(fold_dve, 1)
            dve.wait_ge(fold_dve, 10)
            nc.vector.tensor_tensor(bn[:, 7, :], beta[:, :], bn[:, 6, :], ALU.subtract).then_inc(fold_dve, 1)
            dve.wait_ge(fold_dve, 12)
            nc.vector.tensor_copy(bv_wide[:, :], bn[:, 7, 2:3].to_broadcast([P, P])).then_inc(fold_dve, 1)
            dve.wait_ge(fold_pe, 4)
            nc.vector.tensor_copy(mix[:, :], bank[3][:, 0:D]).then_inc(fold_dve, 1)
            dve.wait_ge(fold_pe, 6)
            nc.vector.tensor_copy(mix_bias[:, :], bank[4][:, 0:1]).then_inc(fold_dve, 1)
            nc.vector.tensor_copy(outw[:, 0, :], bank[5][:, 0:D]).then_inc(fold_dve, 1)
            dve.wait_ge(fold_pe, 7)
            nc.vector.tensor_copy(outw[:, 1, :], bank[6][:, 0:D]).then_inc(fold_dve, 1)
            dve.wait_ge(fold_dve, 17)

            def body(h, k):
                if s := stage(h, k, 1, B):
                    n, _, kk = s
                    dve.wait_ge(exp_done, 2 * n + 2)
                    need(dve, f_ready, 2 * (n - 1))
                    nc.vector.reciprocal(rsums[:, kk, :], psums[:, kk, :]).then_inc(rsums_done, 1)
                if s := stage(h, k, 0, B):
                    n, _, kk = s
                    dve.wait_ge(scores_done, n + 1)
                    for j, (lo, hi) in enumerate(((0, P), (P, 384))):
                        nc.vector.tensor_reduce(top[:, kk, j:j + 1], bank[1 + kk][:, lo:hi], AX,
                                                ALU.max).then_inc(max_step, 1)
                    dve.wait_ge(max_step, PER_MAX * n + 2)
                    nc.vector.tensor_scalar(nbias[:, kk, :], top[:, kk, :], -SCALE, None, ALU.mult).then_inc(max_step, 1)
                if s := stage(h, k, 2, B):
                    n, _, kk = s
                    dve.wait_ge(f_done, n + 1)
                    dve.wait_ge(rsums_done, n + 1)
                    for j in range(2):
                        nc.vector.scalar_tensor_tensor(
                            out=f[:, kk, j, :], in0=bank[5][:, j * D:(j + 1) * D], scalar=rsums[:, kk, j:j + 1],
                            in1=outw[:, 1, :], op0=ALU.mult, op1=ALU.add).then_inc(f_ready, 1)
                if s := stage(h, k, 3, B):
                    n, _, kk = s
                    dve.wait_ge(norm_pow, n + 1)
                    for j in range(2):
                        xt = x_sb[:, ds(2 * n + j, 1), :].rearrange("p a d -> p (a d)")
                        nc.vector.scalar_tensor_tensor(out=xt, in0=f[:, kk, j, :], scalar=rstd2[:, kk, j:j + 1],
                                                       in1=xt, op0=ALU.mult, op1=ALU.add).then_inc(x2_ready, 1)
                    for j in range(2):
                        dve.wait_ge(x2_ready, 2 * n + 1 + j)
                        dve.sem_inc(dve_waited, 1)
                        nc.vector.bn_stats(stat2[:, 1 - kk, j, :],
                                           x_sb[:, ds(2 * n + j, 1), :].rearrange("p a d -> p (a d)")).then_inc(x2_stats, 1)
                if s := stage(h, k, 2, B + 2):
                    n, _, kk = s
                    if not isinstance(n, int) or 0 < n <= B:
                        dve.wait_ge(x2_stats, 2 * n)
                    need(dve, xr_less_mean, n - 2)
                    dve.sem_inc(dve_waited, 1)
                    for j in range(2):
                        nc.vector.bn_aggr(mv2[:, kk, j, :], stat2[:, kk, j, :]).then_inc(norm_aggr, 1)
                    dve.wait_ge(norm_aggr, 2 * n + 2)
                    need(dve, norm_pow, n - 1)
                    nc.vector.tensor_scalar(veps2[:, kk, 2:4], mv2[:, kk, :, 1], EPS, None, ALU.add).then_inc(norm_var, 1)
                if isinstance(h, int) and 2 * h + k == SOFT_STEP:
                    soft_less_max(0)
                if isinstance(h, int) and 2 * h + k == SOFT_STEP + 1:
                    soft_divide(0)

            def soft_less_max(p):
                lo, hi = SOFT[p]
                dve.wait_ge(logits_done, hi // 2)
                lg = bank[(7, 0)[p]][:, 0:(hi - lo) * E].rearrange("p (t e) -> p t e", e=E)
                nc.vector.tensor_reduce(rmax[:, lo:hi], lg, AX, ALU.max).then_inc(soft_dve[p], 1)
                dve.wait_ge(soft_dve[p], 1)
                nc.vector.tensor_tensor(logit[:, lo:hi, :], lg, rmax[:, lo:hi].unsqueeze(2).to_broadcast([P, hi - lo, E]),
                                        ALU.subtract).then_inc(soft_dve[p], 1)

            def soft_divide(p):
                lo, hi = SOFT[p]
                dve.wait_ge(soft_exp[p], 1)
                nc.vector.tensor_reduce(rsum[:, lo:hi], logit[:, lo:hi, :], AX, ALU.add).then_inc(soft_dve[p], 1)
                dve.wait_ge(soft_dve[p], 3)
                nc.vector.reciprocal(rinv[:, lo:hi], rsum[:, lo:hi]).then_inc(soft_dve[p], 1)
                dve.wait_ge(soft_dve[p], 4)
                nc.vector.tensor_tensor(score[:, lo:hi, :], logit[:, lo:hi, :],
                                        rinv[:, lo:hi].unsqueeze(2).to_broadcast([P, hi - lo, E]),
                                        ALU.mult).then_inc(soft_dve[p], 1)

            pipeline(dve, body, A_STEPS, A_LO, A_HI)

            soft_less_max(1)
            soft_divide(1)

            dve.wait_ge(consts_ready, 2)
            nc.vector.tensor_scalar(digit_clamped[:, :, :], digit_shift[:, :, :], 0.0, None,
                                    ALU.max).then_inc(search_step, 1)
            dve.wait_ge(search_step, 1)
            nc.vector.tensor_tensor(digit_bits[:, :, :], digits[:, :, :], digit_clamped[:, :, :],
                                    ALU.logical_shift_left).then_inc(search_step, 1)
            dve.wait_ge(search_step, 2)
            nc.vector.memset(digit_bits[:, DIGITS:, :], 0).then_inc(search_step, 1)
            nc.vector.tensor_copy(cand[:, 0, :], digit_bits[:, 0, :]).then_inc(search_step, 1)
            nc.vector.memset(count[:, 3:7], float(CAP)).then_inc(search_step, 1)
            for side, digits_there, op in ((0, slice(0, LEFT), ALU.logical_shift_left),
                                           (1, slice(LEFT, DIGITS), ALU.logical_shift_right)):
                nc.vector.tensor_tensor(four_bits[:, digits_there, :], four[:, digits_there, :].bitcast(I32),
                                        place_shift[:, side, digits_there, :], op).then_inc(search_step, 1)
            dve.wait_ge(search_step, 3)
            nc.vector.tensor_tensor(digit_flip[:, :, :], digit_bits[:, 0:DIGITS, :], digit_bits[:, 1:, :],
                                    ALU.bitwise_xor).then_inc(search_step, 1)
            dve.wait_ge(search_step, 8)
            nc.vector.tensor_tensor(digit_flip[:, :, :], digit_flip[:, :, :], four_bits[:, :, :],
                                    ALU.bitwise_xor).then_inc(search_step, 1)
            dve.wait_ge(by_expert_ready, 1)
            nc.vector.tensor_copy(upper[:, :], by_expert[:, :].bitcast(BF16).rearrange("p (a b) -> p a b", b=2)[:, :, 1]
                                  ).then_inc(upper_ready, 1)
            dve.wait_ge(upper_ready, 1)
            FIRST, PER = 9, 3

            def search(i, k, side, scores=by_expert):
                dve.wait_ge(search_step, FIRST + PER * i)
                for j in range(3):
                    last = nc.vector.tensor_scalar(hits[:, j, :], scores[:, :], cand[:, k, j:j + 1].bitcast(F32), None,
                                                   ALU.is_ge, ALU.add, accum_out=count[:, j:j + 1])
                last.then_inc(counted, 1)
                nc.vector.tensor_tensor(cand_next[:, :], cand[:, k, :],
                                        digit_flip[:, ds(i, 1), :].rearrange("p a j -> p (a j)"),
                                        ALU.bitwise_xor).then_inc(search_step, 1)
                dve.wait_ge(counts_summed, i + 1)
                nc.vector.tensor_scalar(enough[:, :], bank[6][:, 0:7], float(CAP), None,
                                        ALU.is_ge, ALU.add, accum_out=four_plus_digit[:, :]).then_inc(search_step, 1)
                dve.wait_ge(search_step, FIRST + PER * i + 2)
                nc.vector.scalar_tensor_tensor(out=cand[:, 1 - k, :],
                                               in0=four_plus_digit[:, :].bitcast(I32).to_broadcast([P, 3]),
                                               scalar=place_shift[:, side, ds(i, 1), 0], in1=cand_next[:, :],
                                               op0=(ALU.logical_shift_left, ALU.logical_shift_right)[side],
                                               op1=ALU.bitwise_xor).then_inc(search_step, 1)

            for i in range(UPPER):
                search(i, i % 2, 0 if i < LEFT else 1, upper)
            search(UPPER, UPPER % 2, 1)
            with dve.Fori((UPPER + 1) // 2, DIGITS // 2) as h:
                for k in range(2):
                    search(2 * h + k, k, 1)
            search(DIGITS - 1, 0, 1)
            dve.wait_ge(search_step, FIRST + PER * DIGITS)

            def ranks():
                nc.vector.tensor_copy(least_wide[0:E, :],
                                      cand[0:E, 1, 0:1].bitcast(F32).to_broadcast([E, P])).then_inc(rank_dve, 1)
                dve.wait_ge(rank_pe, 1)
                nc.vector.tensor_copy(least[:, :], bank[0][:, 0:E]).then_inc(rank_dve, 1)
                dve.wait_ge(rank_dve, 2)
                dve.wait_ge(chunks_loaded, 16)
                ch = chunked[:, :, :].rearrange("p j e -> p e j")
                lw = least[:, :].unsqueeze(2).to_broadcast([P, E, 32])
                nc.vector.tensor_tensor(above[:, :, :], ch, lw, ALU.is_gt).then_inc(rank_dve, 1)
                nc.vector.tensor_tensor(equal[:, :, :], ch, lw, ALU.is_equal).then_inc(rank_dve, 1)

                def flat(a):
                    return a[:, :, :].rearrange("p e j -> p (e j)")

                for i, (src, dst) in enumerate(((above, above_sum), (equal, equal_sum))):
                    dve.wait_ge(rank_dve, 3 + i)
                    nc.vector.tensor_tensor_scan(flat(dst), flat(scan_keep), flat(src), 0.0,
                                                 ALU.mult, ALU.add).then_inc(rank_dve, 1)
                dve.wait_ge(rank_pe, 2)
                nc.vector.tensor_scalar(wanted[:, :], bank[7][:, 2 * E:3 * E], -1.0, float(CAP), ALU.mult,
                                        ALU.add).then_inc(rank_dve, 1)
                dve.wait_ge(rank_dve, 7)
                nc.vector.tensor_tensor(equal_before[:, :], bank[7][:, E:2 * E], wanted[:, :], ALU.min).then_inc(rank_dve, 1)
                dve.wait_ge(rank_dve, 8)
                nc.vector.tensor_tensor(wanted_here[:, :], wanted[:, :], equal_before[:, :],
                                        ALU.subtract).then_inc(rank_dve, 1)
                nc.vector.tensor_tensor(chunk_base[:, :], bank[7][:, 0:E], equal_before[:, :], ALU.add).then_inc(rank_dve, 1)
                dve.wait_ge(rank_dve, 9)
                nc.vector.tensor_tensor(equal_taken[:, :, :], equal_sum[:, :, :],
                                        wanted_here[:, :].unsqueeze(2).to_broadcast([P, E, 32]),
                                        ALU.min).then_inc(rank_dve, 1)
                dve.wait_ge(rank_pe, 4)
                nc.vector.tensor_copy(first_rank[:, :], bank[6][:, 0:E]).then_inc(rank_dve, 1)
                dve.wait_ge(rank_dve, 12)

            ranks()

            def start_slots(s):
                n, _, k = s
                need(dve, looked_up, n - 1)
                nc.vector.tensor_scalar(started[:, k % 2, :], slot_row[:, :], first_rank[:, ds(n, 1)], None,
                                        ALU.is_ge).then_inc(started_ready, 1)

            def index(s):
                n, h, k4 = s
                dve.wait_ge(looked_up, n + 1)
                lk = bank[0][:, 0:NS * 33].rearrange("p (t j) -> p t j", j=33)
                nc.vector.tensor_tensor(passed[:, :, :], lk[:, :, 0:32], slot_col[:, :, :], ALU.is_le).then_inc(idx_step, 1)
                dve.wait_ge(idx_step, PER_IDX * n + 1)
                nc.vector.tensor_reduce(passed_sum[:, :], passed[:, :, :], AX, ALU.add).then_inc(idx_step, 1)
                dve.wait_ge(idx_step, PER_IDX * n + 2)
                nc.vector.scalar_tensor_tensor(out=idx_f[:, :], in0=lk[:, :, 32], scalar=32.0, in1=passed_sum[:, :],
                                               op0=ALU.mult, op1=ALU.add).then_inc(idx_step, 1)
                dve.wait_ge(idx_step, PER_IDX * n + 3)
                nc.vector.tensor_scalar(idx_in[:, k4, :], idx_f[:, :], -32.0, None, ALU.add).then_inc(idx_step, 1)

            def keep_scores(s):
                n, h, k4 = s
                dve.wait_ge(gathered[k4 % 2], 16 * NS * (2 * h + k4 // 2 + 1))
                need(dve, eo_scaled, 2 * (n - 3))
                nc.vector.tensor_scalar(weight[:, k4, :].unsqueeze(2), xg[:, k4 % 2, :, ds(D + n, 1)], 1.0 / W_UP, None,
                                        ALU.mult).then_inc(kept, 1)

            def weights_lo(s):
                n, _, k4 = s
                k = k4 % 2
                dve.wait_ge(gu_hi_ready, n + 1)
                need(dve, up_done, IC * (n - 1))
                nc.vector.scalar_tensor_tensor(out=w_gu_lo[:, k, :], in0=w_gu[:, k, :], scalar=W_UP,
                                               in1=w_gu_hi[:, k, :], op0=ALU.mult,
                                               op1=ALU.subtract).then_inc(gu_lo_ready, 1)

            def tokens_lo(s):
                n, _, k4 = s
                k = k4 % 2
                dve.wait_ge(xgT_hi_ready, n + 1)
                need(dve, up_done, IC * (n - 1))
                nc.vector.tensor_tensor(xgT_lo[:, k, :], bank[1][:, :], xgT_hi[:, k, :],
                                        ALU.subtract).then_inc(xgT_lo_ready, 1)

            def scale_out(s):
                n, h, k4 = s
                k = k4 % 2
                if isinstance(n, int) and n == E - 1:
                    dve.wait_ge(scattered[k], 16 * NS * (E // 2 - 1))
                    nc.vector.tensor_copy(idx_out[:, k4, :], idx_in[:, k4, :]).then_inc(tail_scaled, 1)
                    for t in range(NS):
                        dve.wait_ge(tail_done, t + 1)
                        dve.wait_ge(kept, E)
                        nc.vector.tensor_scalar(eo[:, k, t, :], bank[2 + t][:, 0:D],
                                                weight[:, k4, t:t + 1], None, ALU.mult).then_inc(tail_scaled, 1)
                    return
                dve.wait_ge(eo_done, n + 1)
                dve.wait_ge(kept, n + 1)
                need(dve, scattered[k], 16 * NS * (2 * h + k4 // 2))
                nc.vector.tensor_copy(idx_out[:, k4, :], idx_in[:, k4, :]).then_inc(eo_scaled, 1)
                nc.vector.tensor_tensor(eo[:, k, :, :], bank[6 + k][:, :].rearrange("p (t d) -> p t d", d=D),
                                        weight[:, k4, :].unsqueeze(2).to_broadcast([P, NS, D]),
                                        ALU.mult).then_inc(eo_scaled, 1)

            def experts(h, k):
                this, following = stage(h, k, 0, E, E_TURN), stage(h, k, -1, E, E_TURN)
                later = stage(h, k, -3, E, E_TURN)

                def hidden(c):
                    if this:
                        n, _, kk = this
                        if c == 0:
                            need(dve, eo_done, n - 1)
                        dve.wait_ge(gelu_done, IC * n + c + 1)
                        dve.wait_ge(up_done, IC * n + c + 1)
                        nc.vector.tensor_tensor(hid[:, kk % 2, c, :], gelu[:, c % 2, :], bank[4 + c % 2][:, :],
                                                ALU.mult).then_inc(hid_done, 1)

                hidden(0)
                if later:
                    start_slots(later)
                if following:
                    weights_lo(following)
                if s := stage(h, k, 1, E, E_TURN):
                    scale_out(s)
                hidden(1)
                if following:
                    tokens_lo(following)
                    keep_scores(following)
                hidden(2)
                hidden(3)
                if later:
                    index(later)

            for n in range(2):
                start_slots((n, 0, n))
            index((0, 0, 0))
            start_slots((2, 0, 2))
            for n in range(1, 3):
                index((n, 0, n))
            weights_lo((0, 0, 0))
            tokens_lo((0, 0, 0))
            keep_scores((0, 0, 0))
            pipeline(dve, experts, E + 1, E_LO, E_HI, E_TURN)

            def last_norm(h, j):
                g = 4 * h + j
                k = j % 2
                dve.wait_ge(sum_loaded[j], 16 * (h + 1))
                for i in range(4):
                    nc.vector.bn_stats(stat[:, k, i, :],
                                       acc_sb[:, ds(4 * g + i, 1), :].rearrange("p a d -> p (a d)")).then_inc(fin_step, 1)
                dve.wait_ge(fin_step, 8 * g + 4)
                dve.sem_inc(dve_waited, 1)
                for i in range(4):
                    nc.vector.bn_aggr(mv[:, k, i, :], stat[:, k, i, :]).then_inc(fin_step, 1)
                if not isinstance(g, int) or g >= 1:
                    last_shift(g - 1, 1 - k)
                dve.wait_ge(fin_step, 8 * (g + 1))
                nc.vector.tensor_scalar(veps[:, k, :], mv[:, k, :, 1], EPS, None, ALU.add).then_inc(fin_var, 1)
                if not isinstance(g, int) or g >= 2:
                    last_add(g - 2)

            def last_shift(g, k):
                dve.wait_ge(fin_pow, g + 1)
                need(dve, fin_normed, 4 * (g - 1))
                nc.vector.scalar_tensor_tensor(out=shiftm[:, k, :], in0=mv[:, k, :, 0], scalar=-1.0, in1=rstd[:, k, :],
                                               op0=ALU.mult, op1=ALU.mult).then_inc(fin_shift, 1)

            def last_add(g):
                dve.wait_ge(fin_normed, 4 * g + 4)
                t = ds(4 * g + 2, 2)
                nc.vector.tensor_tensor(x_sb[:, t, :], x_sb[:, t, :], acc_sb[:, t, :], ALU.add).then_inc(fin_ready_dve, 1)

            for g in range(4):
                last_norm(0, g)
            with dve.Fori(1, NG // 4) as h:
                for j in range(4):
                    last_norm(h, j)
            last_shift(NG - 1, (NG - 1) % 2)
            last_add(NG - 2)
            last_add(NG - 1)


def kernel(**inputs):
    import numpy as np
    import concourse.bacc as bacc
    from concourse.bass_utils import run_bass_kernel_spmd

    a = {k: np.asarray(v) for k, v in inputs.items()}
    x = a["L0_attn_x"]
    wg, wu, wd = a["L0_ffn_Wg"], a["L0_ffn_Wu"], a["L0_ffn_Wd"]
    n_exp, hidden, d = wg.shape
    down = wd.transpose(0, 2, 1).reshape(n_exp, hidden // P, P, d).transpose(0, 2, 1, 3).reshape(n_exp, P, hidden)
    shared_down = a["L0_ffn_Sd"].T.reshape(-1, P, d).transpose(1, 0, 2).reshape(P, -1)
    arrays = {
        "x": x.reshape(-1, d),
        "low_rank": np.concatenate([a["L0_attn_lora_attn_A"].T, a["L0_attn_lora_attn_B"], a["L0_attn_lora_proj_A"].T,
                                    a["L0_attn_lora_proj_B"]], axis=1),
        "attn_w": np.concatenate([a["L0_attn_W_attn"].reshape(d, 3 * d), a["L0_attn_W_proj"],
                                  a["L0_attn_bn_gamma"].reshape(3, d).T, a["L0_attn_bn_beta"].reshape(3, d).T], axis=1),
        "ffn_w": np.concatenate([a["L0_ffn_Sg"].T, a["L0_ffn_Su"].T, shared_down, a["L0_ffn_gate_w"].T], axis=1),
        "w_experts": np.concatenate([wg.transpose(0, 2, 1), wu.transpose(0, 2, 1), down], axis=2),
    }
    arrays = {k: np.ascontiguousarray(v) for k, v in arrays.items()}
    nc = bacc.Bacc("TRN2", target_bir_lowering=False, num_devices=1)
    args = {k: nc.dram_tensor(f"in_{k}", v.shape, mybir.dt.from_np(v.dtype), kind="ExternalInput").ap()
            for k, v in arrays.items()}
    out = nc.dram_tensor("out", (x.shape[0] * x.shape[1], d), F32, kind="ExternalOutput").ap()
    build(nc, *args.values(), out)
    r = run_bass_kernel_spmd(nc, [{f"in_{k}": v for k, v in arrays.items()}], core_ids=[0])
    return r.results[0]["out"].reshape(x.shape)
```
